# Optimizing a Trainium2 kernel written in Bass

```python
import numpy as np
import jax
import jax.numpy as jnp

def _softmax(x, axis=-1):
    return jax.nn.softmax(x, axis=axis)

def _gelu(x):
    return jax.nn.gelu(x, approximate=True)

def _silu(x):
    return jax.nn.silu(x)

def _sigmoid(x):
    return jax.nn.sigmoid(x)

def _layernorm(x, axis=-1, eps=1e-05):
    m = jnp.mean(x, axis=axis, keepdims=True)
    v = jnp.var(x, axis=axis, keepdims=True)
    return (x - m) / jnp.sqrt(v + eps)

def _scatter_add(tgt, idx, src, axis=0):
    return tgt.at[idx].add(src)

def _segment_sum(src, seg, n):
    return jax.ops.segment_sum(src, seg, n)
kernel_name = 'mk_lm_tower_d1_tok_ids512_r4_8582a1'

def setup_inputs(seed: int=0):
    np.random.seed(seed)
    _w = jnp.asarray

    def _rec_inputs():
        import jax
        import jax.numpy as jnp
        _rk = jax.random.key(seed)
        x = jax.random.randint(jax.random.fold_in(_rk, 1), (8, 256), 0, 8000, jnp.int32)
        return x
    x = _rec_inputs()

    def _L0_tok_setup():
        import jax, jax.numpy as jnp
        import numpy as np
        VOCAB = 8000
        DIM = 128
        PAD_IDX = 0
        key = jax.random.key(seed)
        k_tok, k_w = jax.random.split(key)
        tensor = jax.random.randint(k_tok, (16, 512), 0, VOCAB, dtype=jnp.int64)
        weight = jax.random.normal(k_w, (VOCAB, DIM), dtype=jnp.float32)
        weight = weight.at[PAD_IDX].set(0.0)
        return {'tensor': tensor, 'weight': weight}
    _L0_tok_all = _L0_tok_setup()
    _L0_tok_in = {k: v for k, v in _L0_tok_all.items() if k in ('weight',)}
    del _L0_tok_all

    def _L0_attn_setup():
        import jax, jax.numpy as jnp
        import numpy as np
        H, DH, M, DIN = (8, 64, 32, 128)
        INNER = H * DH
        key = jax.random.key(seed)
        ks = jax.random.split(key, 12)
        s = 0.02
        B, N = (4, 4096)
        return {'x': jax.random.normal(ks[0], (B, N, DIN), jnp.float32), 'Wx': jax.random.normal(ks[1], (INNER, DIN), jnp.float32) * s, 'bx': jnp.zeros((INNER,), jnp.float32), 'Wfx': jax.random.normal(ks[2], (INNER, DIN), jnp.float32) * s, 'bfx': jnp.zeros((INNER,), jnp.float32), 'Wslice': jax.random.normal(ks[3], (M, DH), jnp.float32) * s, 'bslice': jnp.zeros((M,), jnp.float32), 'Wq': jax.random.normal(ks[4], (DH, DH), jnp.float32) * s, 'Wk': jax.random.normal(ks[5], (DH, DH), jnp.float32) * s, 'Wv': jax.random.normal(ks[6], (DH, DH), jnp.float32) * s, 'Wout': jax.random.normal(ks[7], (DIN, INNER), jnp.float32) * s, 'bout': jnp.zeros((DIN,), jnp.float32), 'temperature': jnp.full((1, H, 1, 1), 0.5, jnp.float32)}
    _L0_attn_all = _L0_attn_setup()
    _L0_attn_in = {k: v for k, v in _L0_attn_all.items() if k in ('Wx', 'bx', 'Wfx', 'bfx', 'Wslice', 'bslice', 'Wq', 'Wk', 'Wv', 'Wout', 'bout', 'temperature')}
    del _L0_attn_all

    def _L0_ffn_setup():
        import jax, jax.numpy as jnp
        import numpy as np
        B, S, D, O = (1, 512, 128, 128)
        H, QD, K, PK = (8, 64, 16, 64)
        N = PK * PK
        HALF = QD // 2

        def _l2norm(x):
            n = jnp.sqrt(jnp.sum(x * x, axis=-1, keepdims=True))
            return x / jnp.maximum(n, 1e-12)
        key = jax.random.key(seed)
        ks = jax.random.split(key, 9)
        return {'hidden_states': jax.random.normal(ks[0], (B, S, D), jnp.float32), 'Wq': jax.random.normal(ks[1], (H * QD, D), jnp.float32) * 0.02, 'bq': jnp.zeros((H * QD,), jnp.float32), 'ln_g': jnp.ones((QD,), jnp.float32), 'ln_b': jnp.zeros((QD,), jnp.float32), 'keys0': jax.random.normal(ks[2], (PK, HALF), jnp.float32) * 0.02, 'keys1': jax.random.normal(ks[3], (PK, HALF), jnp.float32) * 0.02, 'expert_down': jax.random.normal(ks[4], (N, D), jnp.float32) * 0.02, 'expert_up': jax.random.normal(ks[5], (N, O), jnp.float32) * 0.02}
    _L0_ffn_all = _L0_ffn_setup()
    _L0_ffn_in = {k: v for k, v in _L0_ffn_all.items() if k in ('Wq', 'bq', 'ln_g', 'ln_b', 'keys0', 'keys1', 'expert_down', 'expert_up')}
    del _L0_ffn_all
    return {'x': x, 'L0_tok_weight': _L0_tok_in['weight'], 'L0_attn_Wx': _L0_attn_in['Wx'], 'L0_attn_bx': _L0_attn_in['bx'], 'L0_attn_Wfx': _L0_attn_in['Wfx'], 'L0_attn_bfx': _L0_attn_in['bfx'], 'L0_attn_Wslice': _L0_attn_in['Wslice'], 'L0_attn_bslice': _L0_attn_in['bslice'], 'L0_attn_Wq': _L0_attn_in['Wq'], 'L0_attn_Wk': _L0_attn_in['Wk'], 'L0_attn_Wv': _L0_attn_in['Wv'], 'L0_attn_Wout': _L0_attn_in['Wout'], 'L0_attn_bout': _L0_attn_in['bout'], 'L0_attn_temperature': _L0_attn_in['temperature'], 'L0_ffn_Wq': _L0_ffn_in['Wq'], 'L0_ffn_bq': _L0_ffn_in['bq'], 'L0_ffn_ln_g': _L0_ffn_in['ln_g'], 'L0_ffn_ln_b': _L0_ffn_in['ln_b'], 'L0_ffn_keys0': _L0_ffn_in['keys0'], 'L0_ffn_keys1': _L0_ffn_in['keys1'], 'L0_ffn_expert_down': _L0_ffn_in['expert_down'], 'L0_ffn_expert_up': _L0_ffn_in['expert_up']}

def reference(x, L0_tok_weight, L0_attn_Wx, L0_attn_bx, L0_attn_Wfx, L0_attn_bfx, L0_attn_Wslice, L0_attn_bslice, L0_attn_Wq, L0_attn_Wk, L0_attn_Wv, L0_attn_Wout, L0_attn_bout, L0_attn_temperature, L0_ffn_Wq, L0_ffn_bq, L0_ffn_ln_g, L0_ffn_ln_b, L0_ffn_keys0, L0_ffn_keys1, L0_ffn_expert_down, L0_ffn_expert_up):
    import jax
    import jax.numpy as jnp

    def _L0_tok_ref(tensor, weight):
        import jax, jax.numpy as jnp
        import numpy as np
        VOCAB = 8000
        DIM = 128
        PAD_IDX = 0
        return jnp.take(weight, tensor, axis=0)

    def _L0_attn_ref(x, Wx, bx, Wfx, bfx, Wslice, bslice, Wq, Wk, Wv, Wout, bout, temperature):
        import jax, jax.numpy as jnp
        import numpy as np
        H, DH, M, DIN = (8, 64, 32, 128)
        INNER = H * DH
        B, N, D = x.shape
        scale = DH ** (-0.5)
        x_mid = (x @ Wx.T + bx).reshape(B, N, H, DH).transpose(0, 2, 1, 3)
        fx_mid = (x @ Wfx.T + bfx).reshape(B, N, H, DH).transpose(0, 2, 1, 3)
        slice_logits = (x_mid @ Wslice.T + bslice) / temperature
        slice_weights = jax.nn.softmax(slice_logits, axis=-1)
        slice_norm = slice_weights.sum(axis=2)
        slice_token = jnp.einsum('bhnd,bhnm->bhmd', fx_mid, slice_weights)
        slice_token = slice_token / (slice_norm[:, :, :, None] + 1e-05)
        q = slice_token @ Wq.T
        k = slice_token @ Wk.T
        v = slice_token @ Wv.T
        attn = jax.nn.softmax(jnp.einsum('bhmd,bhkd->bhmk', q, k) * scale, axis=-1)
        out_slice = jnp.einsum('bhmk,bhkd->bhmd', attn, v)
        out_x = jnp.einsum('bhmd,bhnm->bhnd', out_slice, slice_weights)
        out_x = out_x.transpose(0, 2, 1, 3).reshape(B, N, INNER)
        return out_x @ Wout.T + bout

    def _L0_ffn_ref(hidden_states, Wq, bq, ln_g, ln_b, keys0, keys1, expert_down, expert_up):
        import jax, jax.numpy as jnp
        import numpy as np
        B, S, D, O = (1, 512, 128, 128)
        H, QD, K, PK = (8, 64, 16, 64)
        N = PK * PK
        HALF = QD // 2

        def _l2norm(x):
            n = jnp.sqrt(jnp.sum(x * x, axis=-1, keepdims=True))
            return x / jnp.maximum(n, 1e-12)
        b, s, d = hidden_states.shape
        q = (hidden_states @ Wq.T + bq).reshape(b, s, H, QD)
        mu = jnp.mean(q, axis=-1, keepdims=True)
        var = jnp.mean((q - mu) ** 2, axis=-1, keepdims=True)
        q = (q - mu) / jnp.sqrt(var + 1e-05) * ln_g + ln_b
        q0, q1 = (q[..., :HALF], q[..., HALF:])
        s0 = jnp.einsum('bshq,eq->bshe', _l2norm(q0), _l2norm(keys0))
        s1 = jnp.einsum('bshq,eq->bshe', _l2norm(q1), _l2norm(keys1))
        sc0, ix0 = jax.lax.top_k(s0, K)
        sc1, ix1 = jax.lax.top_k(s1, K)
        cs = (sc0[..., :, None] + sc1[..., None, :]).reshape(b, s, H, K * K)
        ci = (ix0[..., :, None] + ix1[..., None, :]).reshape(b, s, H, K * K)
        fs, pos = jax.lax.top_k(cs, K)
        fi = jnp.take_along_axis(ci, pos, axis=-1)
        w = jax.nn.softmax(fs, axis=-1)
        down = expert_down[fi]
        up = expert_up[fi]
        inner = jnp.einsum('bsd,bshkd->bshk', hidden_states, down)
        act = jax.nn.gelu(inner, approximate=False)
        out = jnp.einsum('bshk,bshko->bso', act * w, up)
        return out
    h = _L0_tok_ref(x, L0_tok_weight)
    h = h + _L0_attn_ref(_layernorm(h, axis=-1), L0_attn_Wx, L0_attn_bx, L0_attn_Wfx, L0_attn_bfx, L0_attn_Wslice, L0_attn_bslice, L0_attn_Wq, L0_attn_Wk, L0_attn_Wv, L0_attn_Wout, L0_attn_bout, L0_attn_temperature)
    h = h + _L0_ffn_ref(_layernorm(h, axis=-1), L0_ffn_Wq, L0_ffn_bq, L0_ffn_ln_g, L0_ffn_ln_b, L0_ffn_keys0, L0_ffn_keys1, L0_ffn_expert_down, L0_ffn_expert_up)
    return h

_drawn_inputs = setup_inputs


def setup_inputs(seed=0):
    import zlib

    import numpy as np

    out = dict(_drawn_inputs(seed))
    spreads = {'L0_attn_bx': (0.0, 0.8),
     'L0_attn_bfx': (0.0, 0.8),
     'L0_attn_bslice': (0.0, 0.8),
     'L0_attn_bout': (0.0, 0.29),
     'L0_attn_temperature': (0.5, 0.6),
     'L0_ffn_bq': (0.0, 0.8),
     'L0_ffn_ln_g': (1.0, 0.6),
     'L0_ffn_ln_b': (0.0, 0.8)}
    factors = {'L0_attn_Wx': 8.0,
     'L0_attn_Wfx': 8.0,
     'L0_attn_Wslice': 8.0,
     'L0_attn_Wq': 8.0,
     'L0_attn_Wk': 8.0,
     'L0_attn_Wv': 7.331,
     'L0_attn_Wout': 7.59,
     'L0_ffn_Wq': 8.0,
     'L0_ffn_keys0': 8.0,
     'L0_ffn_keys1': 8.0,
     'L0_ffn_expert_down': 8.0,
     'L0_ffn_expert_up': 8.0}
    for name, (base, spread) in spreads.items():
        noise = np.random.default_rng([zlib.crc32(name.encode()), seed]).standard_normal(out[name].shape)
        drawn = base * np.exp(spread * noise) if base else spread * noise
        out[name] = jnp.asarray(drawn.astype(out[name].dtype))
    for name, factor in factors.items():
        out[name] = (out[name] * factor).astype(out[name].dtype)
    return out
```

```python
import concourse.bass as bass
import concourse.mybir as mybir
from contextlib import ExitStack


def tower_program(nc, ids, tok, wx, wfxT, wsT, bxT, bfx, bslice, attn_wq, attn_wk, attn_wv, woutT, bout,
                  temperature, ffn_wqT, bq, ln_g, ln_b, keys0, keys1, downT, up, out):
    F32, I32 = mybir.dt.float32, mybir.dt.int32
    ALU, ACT, AX = mybir.AluOpType, mybir.ActivationFunctionType, mybir.AxisListType.X
    ds = bass.ds

    P = 128
    TILES = ids.shape[1]
    D = tok.shape[1]
    TPB = 2
    BATCHES = TILES // TPB
    H = temperature.shape[1]
    DH = wsT.shape[0]
    M = wsT.shape[1]
    HM = H * M
    CH = HM // P
    HPC = H // CH
    INNER = H * DH
    PK = keys0.shape[0]
    HALF = keys0.shape[1]
    K = 16
    HS = 2 * H
    E = 2 * PK
    LO = 16
    HI = E // LO
    EPS = 1e-5

    IDX = 7
    UNIT = float(2 ** 23) * 1000 / 1024
    ONE = float(2 ** 23)
    TOP = 2 ** 31 - 2 ** 24
    LEAST = 2.0 ** -126
    RECTS = [(0, 1, 0, 16), (1, 16, 0, 1), (1, 2, 1, 8), (2, 8, 1, 2), (2, 5, 2, 5)]
    NC = sum((a1 - a0) * (b1 - b0) for a0, a1, b0, b1 in RECTS)

    GRP = 4
    NG = P // GRP // 4

    ctx = ExitStack()
    with ctx:
        def sb(name, shape, dt=F32):
            return ctx.enter_context(nc.sbuf_tensor(name, shape, dt))

        def ps(name, shape=(P, 512)):
            return ctx.enter_context(nc.psum_tensor(name, list(shape), F32))

        def sem(name):
            return ctx.enter_context(nc.semaphore(name))

        ident = sb("ident", [P, P])
        ones = sb("ones", [1, P])
        idx_iota = sb("idx_iota", [P, PK], I32)
        lo_iota = sb("lo_iota", [P, LO])
        hi_iota = sb("hi_iota", [P, HI])
        eps_c = sb("eps_c", [P, HS])
        mhalf_c = sb("mhalf_c", [P, HS])
        top_c = sb("top_c", [P, H], I32)
        one_bias = sb("one_bias", [P, 1])
        exp_bias = sb("exp_bias", [P, 1])
        spare = sb("spare", [P, 2])
        ids_sb = sb("ids_sb", [P, TILES], I32)
        wx_sb = sb("wx_sb", [DH, H, D])
        wfxT_sb = sb("wfxT_sb", [D, INNER])
        wsT_sb = sb("wsT_sb", [DH, M])
        bxT_sb = sb("bxT_sb", [DH, H])
        bfx_sb = sb("bfx_sb", [1, INNER])
        bsl_sb = sb("bsl_sb", [1, M])
        aq_sb = sb("aq_sb", [DH, DH])
        ak_sb = sb("ak_sb", [DH, DH])
        av_sb = sb("av_sb", [DH, DH])
        wout_sb = sb("wout_sb", [DH, H, D])
        bout_sb = sb("bout_sb", [1, D])
        temp_sb = sb("temp_sb", [P, H])
        rtemp = sb("rtemp", [P, H])
        lw = sb("lw", [D, HM])
        lb = sb("lb", [1, HM])
        mqk = sb("mqk", [DH, DH])
        vw = sb("vw", [DH, H, D])
        wqT_sb = sb("wqT_sb", [D, H, DH])
        bq_sb = sb("bq_sb", [1, H, DH])
        g_sb = sb("g_sb", [P, DH])
        b_sb = sb("b_sb", [P, DH])
        wmean = sb("wmean", [P, 2, H])
        wqc = sb("wqc", [D, H, DH])
        bqc = sb("bqc", [1, H, DH])
        wqg = sb("wqg", [D, H, DH])
        bqg = sb("bqg", [1, H, DH])
        k_raw = sb("k_raw", [PK, 2, HALF])
        k_sq = sb("k_sq", [PK, 2, HALF])
        k_ss = sb("k_ss", [PK, 2])
        k_rn = sb("k_rn", [PK, 2])
        k_unit = sb("k_unit", [PK, 2, 2, HALF])
        kb = sb("kb", [P, 4, PK])
        downT_sb = sb("downT_sb", [D, E])
        up_sb = sb("up_sb", [E, D])

        h_all = sb("h_all", [P, TILES, D])
        gate = sb("gate", [P, TILES, E])

        a_st = sb("a_st", [P, TPB, 6])
        a_mv = sb("a_mv", [P, TPB, 2])
        a_rs = sb("a_rs", [P, TPB])
        a_x = sb("a_x", [P, TPB, D + 1])
        a_xT = sb("a_xT", [P, TPB, P])
        a_mx = sb("a_mx", [P, TPB * H])
        a_e = sb("a_e", [P, TPB * H, M])
        a_sum = sb("a_sum", [P, TPB * H])
        a_rsum = sb("a_rsum", [P, TPB * H])
        a_sw = sb("a_sw", [P, TPB, HM])
        a_swT = sb("a_swT", [P, CH, TPB * P])
        a_den = sb("a_den", [P, CH])
        a_rden = sb("a_rden", [P, CH])
        a_sn = sb("a_sn", [P, CH, D + 1])
        a_snT = sb("a_snT", [P, HM])
        a_nnT = sb("a_nnT", [1, HM])
        a_stT = sb("a_stT", [DH, HM])
        a_uT = sb("a_uT", [DH, HM])
        a_sv = sb("a_sv", [P, CH, D])
        a_smx = sb("a_smx", [P, CH])
        a_se = sb("a_se", [P, CH, M])
        a_ssum = sb("a_ssum", [P, CH])
        a_srs = sb("a_srs", [P, CH])
        a_at = sb("a_at", [P, CH, M])
        a_atT = sb("a_atT", [P, CH, M])
        a_p = sb("a_p", [P, CH, D])

        l_st = sb("l_st", [P, 6])
        l_mv = [sb(f"l_mv{k}", [P, 2]) for k in range(2)]
        l_rs = [sb(f"l_rs{k}", [P, 1]) for k in range(2)]
        x2 = [sb(f"x2_{k}", [P, D]) for k in range(2)]
        x2T = [sb(f"x2T_{k}", [P, P]) for k in range(2)]
        q_sq = sb("q_sq", [P, H, DH])
        q_ss = sb("q_ss", [P, H])
        q_t = sb("q_t", [P, H])
        q_rs = sb("q_rs", [P, H])
        q_r = sb("q_r", [P, H, DH])
        q_1 = sb("q_1", [P, H, DH])
        q_sq2 = sb("q_sq2", [P, HS, HALF])
        q_ss2 = sb("q_ss2", [P, HS])
        q_t2 = sb("q_t2", [P, HS])
        q_rn = sb("q_rn", [P, HS])
        q_n = sb("q_n", [P, HS, HALF])
        q_nT = sb("q_nT", [P, 4, P])
        y = [sb(f"y{k}", [P, HS * PK], I32) for k in range(2)]

        key = sb("key", [P, HS, PK])
        keym = sb("keym", [P, HS, PK])
        best = [sb(f"best{k}", [P, HS, K]) for k in range(2)]
        base = [sb(f"base{k}", [P, HS], I32) for k in range(2)]
        based = sb("based", [P, H], I32)
        rel = sb("rel", [P, HS, K], I32)
        cand = sb("cand", [P, H, NC], I32)
        candc = sb("candc", [P, H, NC])
        candm = sb("candm", [P, H, NC])
        win = sb("win", [P, H, K])
        valb = sb("valb", [P, H * K], I32)
        hlb = sb("hlb", [P, 2, H * K], I32)
        wexp = [sb(f"wexp{k}", [P, H, K]) for k in range(2)]
        hl = [sb(f"hl{k}", [P, 2, H * K]) for k in range(2)]
        wsum = sb("wsum", [P, H])
        wrec = sb("wrec", [P, H])
        wn = sb("wn", [P, H, K])
        t3 = sb("t3", [P, 3, P])
        ohl = sb("ohl", [P, P, LO])
        ohh = sb("ohh", [P, P // GRP, HI, GRP])
        ohw = sb("ohw", [P, P // GRP, HI, GRP])
        sct = sb("sct", [P, NG, GRP * LO])
        wacc = [sb(f"wacc{k}", [P, E]) for k in range(2)]
        act = sb("act", [P, E])
        actT = sb("actT", [P, P])
        res = [sb(f"res{k}", [P, D]) for k in range(2)]

        pA, pB, pC = ps("pA"), ps("pB"), ps("pC")
        pM = ps("pM")
        pQ = ps("pQ")
        pS = ps("pS", [P, 1024])
        pT = ps("pT")

        loaded = sem("loaded"); ids_in = sem("ids_in"); gathered0 = sem("gathered0"); gathered = sem("gathered")
        pc = sem("pc"); setup_v = sem("setup_v"); setup_p = sem("setup_p"); setup_t = sem("setup_t")
        setup_a = sem("setup_a")
        A = {n: sem("a_" + n + "_done") for n in (
            "st", "mv", "t", "rs", "x", "xTp", "xT", "lg", "mx", "sub", "exp", "sum", "rsum", "sw", "s", "swTp", "swT",
            "den", "rden", "sn", "snTp", "snT", "stp", "stT", "up", "uT", "scp", "smx", "ssub", "sexp", "ssum",
            "srs", "at", "atT", "pp", "p", "op", "h2")}
        F = {n: sem("f_" + n + "_done") for n in (
            "st", "mv", "t", "rs", "x2", "x2Tp", "x2T", "q", "inner", "sq", "gate", "ss", "t1", "t2", "rq", "qr", "q1",
            "sq2", "ss2", "t3", "rn", "qn", "qnTp", "qnT", "sc", "y")}
        S = {n: sem("s_" + n + "_done") for n in (
            "key", "first", "mask", "second", "base", "based", "rel", "cand", "clamp", "wfirst", "wmask", "wsecond",
            "dec", "wexp", "hl", "wsum", "wrec", "wn", "t3p", "t3", "ohl", "ohh", "ohw", "sctp", "sct",
            "act", "actTp", "actT", "mix", "res")}
        spilled = sem("spilled")
        wacc_in = [sem(f"wacc_in{k}") for k in range(2)]
        stored = [sem(f"stored{k}") for k in range(2)]

        LOADS = [(wx_sb[:, :, :], wx.rearrange("(h d) i -> d h i", d=DH)), (wsT_sb[:, :], wsT), (bxT_sb[:, :], bxT),
                 (bsl_sb[:, :], bslice), (temp_sb[:, :], temperature.partition_broadcast(P)),
                 (aq_sb[:, :], attn_wq), (ak_sb[:, :], attn_wk), (av_sb[:, :], attn_wv),
                 (wout_sb[:, :, :], woutT.rearrange("(h i) o -> i h o", i=DH)), (wfxT_sb[:, :], wfxT),
                 (bfx_sb[:, :], bfx), (bout_sb[:, :], bout),
                 (wqT_sb[:, :, :], ffn_wqT.rearrange("p (h d) -> p h d", d=DH)),
                 (bq_sb[:, :, :], bq.rearrange("p (h d) -> p h d", d=DH)),
                 (g_sb[:, :], ln_g.partition_broadcast(P)), (b_sb[:, :], ln_b.partition_broadcast(P)),
                 (k_raw[:, 0, :], keys0), (k_raw[:, 1, :], keys1), (downT_sb[:, :], downT), (up_sb[:, :], up[0:E, :])]
        ALL_LOADED = 16 * len(LOADS)

        FIRST, LAST = -1, BATCHES + 1
        LOOP0, LOOP1 = 3, BATCHES - 1

        def by_group(row):
            return row.rearrange("p (g n) -> p n g", g=GRP).unsqueeze(2).broadcast_to([P, P // GRP, HI, GRP])

        def stages(i, k):
            if i is None:
                return True, True, True, True, True, True
            t = [2 * i + k - n for n in range(5)]
            return (i + 1 < BATCHES, *[0 <= x < TILES for x in t])

        scratch = [nc.dram_tensor(f"scratch{k}", [P, E], F32, kind="Internal").ap() for k in range(2)]
        block = ctx.enter_context(nc.Block())

        @block.sync
        def _(sp):
            sp.dma_start(ids_sb[:, :], ids).then_inc(ids_in, 16)
            for dst, src in LOADS:
                sp.dma_start(dst, src).then_inc(loaded, 16)

            def slot(i, k, on):
                _, _, _, _, sc_on, mix_on = on
                t3_, t4 = 2 * i + k - 3, 2 * i + k - 4
                if mix_on:
                    sp.wait_ge(S["res"], t4 + 1)
                    sp.dma_start(out[ds(t4 * P, P), :], res[k][:, :]).then_inc(stored[k], 16)
                if sc_on:
                    kk = 1 - k
                    sp.wait_ge(S["sct"], t3_ + 1)
                    sp.wait_ge(S["act"], max(t3_ - 1, 0) if isinstance(t3_, int) else t3_ - 1)
                    for g in range(GRP):
                        sp.dma_start(
                            scratch[kk].rearrange("(g c j) (h l) -> g (j h) c l", g=GRP, c=NG, l=LO)[g],
                            sct[g:P:GRP, :, g * LO:(g + 1) * LO]).then_inc(spilled, 16)
                    sp.wait_ge(spilled, 16 * GRP * (t3_ + 1))
                    sp.dma_start(wacc[kk][:, :], scratch[kk]).then_inc(wacc_in[kk], 16)

            for i in range(FIRST, LOOP0):
                for k in range(2):
                    slot(i, k, stages(i, k))
            with sp.Fori(LOOP0, LOOP1) as i:
                for k in range(2):
                    slot(i, k, stages(None, k))
            for i in range(LOOP1, LAST + 1):
                for k in range(2):
                    slot(i, k, stages(i, k))
            for k in range(2):
                sp.wait_ge(stored[k], 16 * (TILES // 2))

        @block.gpsimd
        def _(gp):
            G = nc.gpsimd
            G.memset(ident[:, :], 0.0).then_inc(pc, 1)
            gp.wait_ge(pc, 1)
            G.affine_select(out=ident[:, :], in_=ident[:, :], compare_op=ALU.not_equal, fill=1.0, base=0,
                            pattern=[[-1, P]], channel_multiplier=1).then_inc(pc, 1)
            gp.wait_ge(ids_in, 16)
            for t in range(TILES):
                G.indirect_dma_start(h_all[:, t, :], None, tok[:, :],
                                     bass.IndirectOffsetOnAxis(ap=ids_sb[:, t:t + 1], axis=0)).then_inc(
                                         gathered0 if t < TPB else gathered, 16)
                if t == TPB - 1:
                    G.iota(idx_iota[:, :], [[1, PK]], 0, 0)
                    G.iota(lo_iota[:, :], [[1, LO]], 0, 0, allow_small_or_imprecise_dtypes=True)
                    G.iota(hi_iota[:, :], [[1, HI]], 0, 0, allow_small_or_imprecise_dtypes=True)
                    G.memset(top_c[:, :], TOP)
                    G.memset(eps_c[:, :], EPS)
                    G.memset(mhalf_c[:, :], -0.5).then_inc(pc, 1)
                    gp.wait_ge(pc, 3)
                    gp.wait_ge(setup_v, 1)
                    G.tensor_tensor(k_rn[:, :], k_ss[:, :], mhalf_c[0:PK, 0:2], ALU.pow).then_inc(setup_p, 1)

            def slot(i, k, on):
                att, q_on, _, pair_on, sc_on, mix_on = on
                b = i + 1
                t0, t2, t3_, t4 = 2 * i + k, 2 * i + k - 2, 2 * i + k - 3, 2 * i + k - 4
                if mix_on:
                    gp.wait_ge(wacc_in[k], 16 * (i - 1))
                    gp.wait_ge(F["gate"], i - 1)
                    gp.wait_ge(S["actTp"], t4)
                    G.tensor_tensor(act[:, :], wacc[k][:, :], gate[:, ds(t4, 1), :], ALU.mult).then_inc(S["act"], 1)
                if q_on:
                    gp.wait_ge(F["mv"], t0 + 1)
                    G.tensor_tensor(l_rs[k][:, :], l_mv[k][:, 1:2], eps_c[:, 0:1], ALU.add).then_inc(F["t"], 1)
                    gp.wait_ge(F["t"], t0 + 1)
                    G.tensor_tensor(l_rs[k][:, :], l_rs[k][:, :], mhalf_c[:, 0:1], ALU.pow).then_inc(F["rs"], 1)
                if att and k == 0:
                    gp.wait_ge(A["mv"], b + 1)
                    G.tensor_tensor(a_rs[:, :], a_mv[:, :, 1], eps_c[:, 0:TPB], ALU.add).then_inc(A["t"], 1)
                    gp.wait_ge(A["t"], b + 1)
                    G.tensor_tensor(a_rs[:, :], a_rs[:, :], mhalf_c[:, 0:TPB], ALU.pow).then_inc(A["rs"], 1)
                if pair_on:
                    bs = base[k][:, :].rearrange("p (h s) -> p h s", s=2)
                    bt = best[k][:, :, :].bitcast(I32).rearrange("p (h s) n -> p h s n", s=2)
                    rl = rel[:, :, :].rearrange("p (h s) n -> p h s n", s=2)
                    gp.wait_ge(S["base"], t2 + 1)
                    G.tensor_tensor(based[:, :], bs[:, :, 1], top_c[:, :], ALU.subtract).then_inc(S["based"], 1)
                    G.tensor_tensor(rl[:, :, 0, :], bt[:, :, 0, :],
                                    bs[:, :, 0:1].broadcast_to([P, H, K]), ALU.subtract)
                    gp.wait_ge(S["based"], t2 + 1)
                    G.tensor_tensor(rl[:, :, 1, :], bt[:, :, 1, :],
                                    based[:, :].unsqueeze(2).broadcast_to([P, H, K]), ALU.subtract
                                    ).then_inc(S["rel"], 1)
                    gp.wait_ge(S["rel"], t2 + 1)
                    gp.wait_ge(S["clamp"], t2)
                    at = 0
                    for n, (a0, a1, b0, b1) in enumerate(RECTS):
                        na, nb = a1 - a0, b1 - b0
                        o = cand[:, :, at:at + na * nb].rearrange("p h (a b) -> p h a b", b=nb)
                        ins = G.tensor_tensor(
                            o, rl[:, :, 0, a0:a1].unsqueeze(3).broadcast_to([P, H, na, nb]),
                            rl[:, :, 1, b0:b1].unsqueeze(2).broadcast_to([P, H, na, nb]), ALU.add)
                        at += na * nb
                    ins.then_inc(S["cand"], 1)
                if sc_on:
                    kk = 1 - k
                    gp.wait_ge(S["wrec"], t3_ + 1)
                    gp.wait_ge(S["wexp"], t3_ + 1)
                    gp.wait_ge(S["t3p"], t3_)
                    G.tensor_tensor(wn[:, :, :], wexp[kk][:, :, :],
                                    wrec[:, :].unsqueeze(2).broadcast_to([P, H, K]), ALU.mult).then_inc(S["wn"], 1)
                if q_on:
                    gp.wait_ge(pc, 3)
                    gp.wait_ge(F["ss"], t0 + 1)
                    G.tensor_scalar(q_t[:, :], q_ss[:, :], 1.0 / DH, EPS, ALU.mult, ALU.add).then_inc(F["t1"], 1)
                    gp.wait_ge(F["t1"], t0 + 1)
                    G.tensor_tensor(q_rs[:, :], q_t[:, :], mhalf_c[:, 0:H], ALU.pow).then_inc(F["rq"], 1)
                    gp.wait_ge(F["qr"], t0 + 1)
                    G.tensor_tensor(q_1[:, :, :], q_r[:, :, :], b_sb[:, :].unsqueeze(1).broadcast_to([P, H, DH]),
                                    ALU.add).then_inc(F["q1"], 1)
                if att and k == 0:
                    gp.wait_ge(A["rsum"], b + 1)
                    G.tensor_tensor(a_sw[:, :, :].rearrange("p t (h m) -> p (t h) m", m=M), a_e[:, :, :],
                                    a_rsum[:, :].unsqueeze(2).broadcast_to([P, TPB * H, M]),
                                    ALU.mult).then_inc(A["sw"], 1)
                if sc_on:
                    gp.wait_ge(S["ohh"], t3_ + 1)
                    gp.wait_ge(S["sctp"], t3_)
                    G.tensor_tensor(ohw[:, :, :, :], ohh[:, :, :, :], by_group(t3[:, 0, :]), ALU.mult).then_inc(S["ohw"], 1)
                if q_on:
                    gp.wait_ge(F["ss2"], t0 + 1)
                    G.tensor_tensor(q_rn[:, :], q_ss2[:, :], mhalf_c[:, :], ALU.pow).then_inc(F["rn"], 1)
                    gp.wait_ge(F["rn"], t0 + 1)
                    G.tensor_tensor(q_n[:, :, :], q_1[:, :, :].rearrange("p h (s d) -> p (h s) d", d=HALF),
                                    q_rn[:, :].unsqueeze(2).broadcast_to([P, HS, HALF]),
                                    ALU.mult).then_inc(F["qn"], 1)

            for i in range(FIRST, LOOP0):
                for k in range(2):
                    slot(i, k, stages(i, k))
            with gp.Fori(LOOP0, LOOP1) as i:
                for k in range(2):
                    slot(i, k, stages(None, k))
            for i in range(LOOP1, LAST + 1):
                for k in range(2):
                    slot(i, k, stages(i, k))

        @block.vector
        def _(dv):
            V = nc.vector
            V.memset(ones[:, :], 1.0)
            V.memset(one_bias[:, :], ONE)
            V.memset(exp_bias[:, :], -float(TOP >> IDX) / UNIT)
            V.memset(kb[:, :, :], 0.0)
            for k in range(TPB):
                V.memset(a_x[:, k, D:D + 1], 1.0)
            dv.wait_ge(loaded, ALL_LOADED)
            V.tensor_tensor(k_sq[:, :, :], k_raw[:, :, :], k_raw[:, :, :], ALU.mult).then_inc(setup_t, 1)
            dv.wait_ge(setup_t, 1)
            V.tensor_reduce(k_rn[:, :], k_sq[:, :, :], AX, ALU.add).then_inc(setup_t, 1)
            dv.wait_ge(setup_t, 2)
            V.tensor_scalar(k_ss[:, :], k_rn[:, :], 1e-24, None, ALU.max).then_inc(setup_v, 1)
            V.reciprocal(rtemp[:, :], temp_sb[:, :])
            V.tensor_reduce(wmean[:, 0, :], wqT_sb[:, :, :], AX, ALU.add)
            V.tensor_reduce(wmean[0:1, 1, :], bq_sb[:, :, :], AX, ALU.add).then_inc(setup_t, 1)
            dv.wait_ge(setup_t, 3)
            V.tensor_scalar(wmean[:, 0, :], wmean[:, 0, :], 1.0 / DH, None, ALU.mult)
            V.tensor_scalar(wmean[0:1, 1, :], wmean[0:1, 1, :], 1.0 / DH, None, ALU.mult).then_inc(setup_t, 1)
            dv.wait_ge(setup_t, 4)
            V.tensor_tensor(wqc[:, :, :], wqT_sb[:, :, :], wmean[:, 0, :].unsqueeze(2).broadcast_to([D, H, DH]),
                            ALU.subtract)
            V.tensor_tensor(bqc[:, :, :], bq_sb[:, :, :], wmean[0:1, 1, :].unsqueeze(2).broadcast_to([1, H, DH]),
                            ALU.subtract).then_inc(setup_t, 1)
            dv.wait_ge(setup_t, 5)
            V.tensor_tensor(wqg[:, :, :], wqc[:, :, :], g_sb[:, :].unsqueeze(1).broadcast_to([D, H, DH]), ALU.mult)
            V.tensor_tensor(bqg[:, :, :], bqc[:, :, :], g_sb[0:1, :].unsqueeze(1).broadcast_to([1, H, DH]),
                            ALU.mult)
            dv.wait_ge(setup_p, 1)
            for s in range(2):
                for r in range(2):
                    V.tensor_scalar(k_unit[:, r, s, :], k_raw[:, s, :], k_rn[:, s:s + 1], None,
                                    ALU.mult).then_inc(setup_v, 1)
            dv.wait_ge(setup_a, 1)
            V.tensor_tensor(lw[:, :].rearrange("p (h m) -> p h m", m=M),
                            pA[:, 0:HM].rearrange("p (h m) -> p h m", m=M),
                            rtemp[:, :].unsqueeze(2).broadcast_to([D, H, M]), ALU.mult)
            V.tensor_tensor(lb[:, :].rearrange("p (h m) -> p h m", m=M),
                            pB[0:1, 0:HM].rearrange("p (h m) -> p h m", m=M),
                            rtemp[0:1, :].unsqueeze(2).broadcast_to([1, H, M]), ALU.mult)
            V.tensor_copy(mqk[:, :], pC[0:DH, 0:DH])
            for n in range(2):
                V.tensor_copy(vw[:, 4 * n:4 * n + 4, :], pS[0:DH, 512 * n:512 * n + 512].rearrange(
                    "p (h o) -> p h o", o=D))
            for n in range(4):
                last = V.tensor_copy(kb[32 * n:32 * n + 32, n, :], pQ[32 * n:32 * n + 32, 0:PK])
            last.then_inc(setup_v, 1)

            def att_stats(b):
                dv.wait_ge(gathered0, 16 * TPB)
                if not isinstance(b, int) or b > 0:
                    dv.wait_ge(gathered, 16 * (TILES - TPB))
                for k in range(TPB):
                    last = V.bn_stats(a_st[:, k, :], h_all[:, ds(b * TPB + k, 1), :])
                last.then_inc(A["st"], 1)
                dv.wait_ge(A["st"], b + 1)
                V.memset(spare[:, 0:1], 0.0)
                for k in range(TPB):
                    last = V.bn_aggr(a_mv[:, k, :], a_st[:, k, :])
                last.then_inc(A["mv"], 1)

            def att_norm(b):
                dv.wait_ge(A["rs"], b + 1)
                for k in range(TPB):
                    last = V.tensor_scalar(a_x[:, k, 0:D], h_all[:, ds(b * TPB + k, 1), :].squeeze(1), a_mv[:, k, 0:1],
                                           a_rs[:, k:k + 1], ALU.subtract, ALU.mult)
                last.then_inc(A["x"], 1)

            lg = pB[:, :].rearrange("p (g m) -> p g m", m=M)

            def att_max(b):
                dv.wait_ge(A["lg"], b + 1)
                V.tensor_reduce(a_mx[:, :], lg, AX, ALU.max).then_inc(A["mx"], 1)

            def att_sub(b):
                dv.wait_ge(A["mx"], b + 1)
                V.tensor_tensor(a_e[:, :, :], lg, a_mx[:, :].unsqueeze(2).broadcast_to([P, TPB * H, M]),
                                ALU.subtract).then_inc(A["sub"], 1)

            def att_sum(b):
                dv.wait_ge(A["exp"], b + 1)
                V.tensor_reduce(a_sum[:, :], a_e[:, :, :], AX, ALU.add).then_inc(A["sum"], 1)

            def att_rsum(b):
                dv.wait_ge(A["sum"], b + 1)
                V.reciprocal(a_rsum[:, :], a_sum[:, :]).then_inc(A["rsum"], 1)

            sl = pC[:, 0:CH * (D + 1)].rearrange("p (c d) -> p c d", d=D + 1)

            def att_token(b):
                dv.wait_ge(A["s"], b + 1)
                V.tensor_scalar(a_den[:, :], sl[:, :, D], EPS, None, ALU.add).then_inc(A["den"], 1)
                dv.wait_ge(A["den"], b + 1)
                V.reciprocal(a_rden[:, :], a_den[:, :]).then_inc(A["rden"], 1)
                dv.wait_ge(A["rden"], b + 1)
                V.tensor_tensor(a_sn[:, :, :], sl, a_rden[:, :].unsqueeze(2).broadcast_to([P, CH, D + 1]),
                                ALU.mult).then_inc(A["sn"], 1)

            scp = pA[:, 256:256 + CH * M].rearrange("p (c m) -> p c m", m=M)

            def att_smax(b):
                dv.wait_ge(A["scp"], b + 1)
                V.tensor_reduce(a_smx[:, :], scp, AX, ALU.max).then_inc(A["smx"], 1)
                dv.wait_ge(A["smx"], b + 1)
                V.tensor_tensor(a_se[:, :, :], scp, a_smx[:, :].unsqueeze(2).broadcast_to([P, CH, M]),
                                ALU.subtract).then_inc(A["ssub"], 1)

            def att_ssum(b):
                dv.wait_ge(A["sexp"], b + 1)
                V.tensor_reduce(a_ssum[:, :], a_se[:, :, :], AX, ALU.add).then_inc(A["ssum"], 1)
                dv.wait_ge(A["ssum"], b + 1)
                V.reciprocal(a_srs[:, :], a_ssum[:, :]).then_inc(A["srs"], 1)

            def att_probs(b):
                dv.wait_ge(A["srs"], b + 1)
                V.tensor_tensor(a_at[:, :, :], a_se[:, :, :], a_srs[:, :].unsqueeze(2).broadcast_to([P, CH, M]),
                                ALU.mult).then_inc(A["at"], 1)
                dv.wait_ge(A["at"], b + 1)
                V.transpose(a_atT[:, :, :].rearrange("p c m -> p (c m)"),
                            a_at[:, :, :].rearrange("p c m -> p (c m)")).then_inc(A["atT"], 1)

            def att_residual(b):
                dv.wait_ge(A["op"], b + 1)
                hb = h_all[:, ds(b * TPB, TPB), :]
                V.tensor_tensor(hb, pB[:, 0:TPB * D].rearrange("p (t d) -> p t d", d=D), hb,
                                ALU.add).then_inc(A["h2"], 1)

            def slot(i, k, on):
                att, q_on, list_on, pair_on, sc_on, mix_on = on
                b = i + 1
                t0 = 2 * i + k
                t1, t2, t3_, t4 = t0 - 1, t0 - 2, t0 - 3, t0 - 4
                kk = 1 - k
                if q_on:
                    dv.wait_ge(A["h2"], i + 1)
                    V.bn_stats(l_st[:, :], h_all[:, ds(t0, 1), :]).then_inc(F["st"], 1)
                if att and k == 0:
                    att_stats(b)
                if q_on:
                    dv.wait_ge(F["st"], t0 + 1)
                    V.memset(spare[:, 1:2], 0.0)
                    V.bn_aggr(l_mv[k][:, :], l_st[:, :]).then_inc(F["mv"], 1)
                if list_on:
                    dv.wait_ge(F["y"], t1 + 1)
                    V.scalar_tensor_tensor(key[:, :, :].bitcast(I32), y[kk][:, :].rearrange("p (l e) -> p l e", e=PK),
                                           IDX, idx_iota[:, :].unsqueeze(1).broadcast_to([P, HS, PK]),
                                           ALU.logical_shift_left, ALU.bitwise_or).then_inc(S["key"], 1)
                if sc_on:
                    dv.wait_ge(S["wexp"], t3_ + 1)
                    V.tensor_reduce(wsum[:, :], wexp[kk][:, :, :], AX, ALU.add).then_inc(S["wsum"], 1)
                if q_on:
                    dv.wait_ge(F["rs"], t0 + 1)
                    V.tensor_scalar(x2[k][:, :], h_all[:, ds(t0, 1), :].squeeze(1), l_mv[k][:, 0:1], l_rs[k][:, :],
                                    ALU.subtract, ALU.mult).then_inc(F["x2"], 1)
                if sc_on:
                    dv.wait_ge(S["wsum"], t3_ + 1)
                    V.reciprocal(wrec[:, :], wsum[:, :]).then_inc(S["wrec"], 1)
                if att and k == 0:
                    att_norm(b)
                if list_on:
                    dv.wait_ge(setup_v, 6)
                    dv.wait_ge(S["key"], t1 + 1)
                    for l in range(HS // 2):
                        V.max(best[kk][:, l, 0:8], key[:, l, :])
                if mix_on:
                    dv.wait_ge(S["mix"], t4 + 1)
                    dv.wait_ge(stored[k], 16 * (i - 2))
                    V.tensor_tensor(res[k][:, :], pT[:, 384:512], h_all[:, ds(t4, 1), :].squeeze(1),
                                    ALU.add).then_inc(S["res"], 1)
                if att and k == 0:
                    att_max(b)
                if list_on:
                    for l in range(HS // 2, HS):
                        last = V.max(best[kk][:, l, 0:8], key[:, l, :])
                    last.then_inc(S["first"], 1)
                if q_on:
                    dv.wait_ge(F["sq"], t0 + 1)
                    V.tensor_reduce(q_ss[:, :], q_sq[:, :, :], AX, ALU.add).then_inc(F["ss"], 1)
                if att and k == 0:
                    att_sub(b)
                if pair_on:
                    dv.wait_ge(S["cand"], t2 + 1)
                    V.tensor_scalar(candc[:, :, :], cand[:, :, :].bitcast(F32), LEAST, None,
                                    ALU.max).then_inc(S["clamp"], 1)
                    dv.wait_ge(setup_v, 6)
                    dv.wait_ge(S["clamp"], t2 + 1)
                    for h in range(H):
                        last = V.max(win[:, h, 0:8], candc[:, h, :])
                    last.then_inc(S["wfirst"], 1)
                if q_on:
                    dv.wait_ge(F["rq"], t0 + 1)
                    V.tensor_tensor(q_r[:, :, :], pS[:, 0:INNER].rearrange("p (h d) -> p h d", d=DH),
                                    q_rs[:, :].unsqueeze(2).broadcast_to([P, H, DH]), ALU.mult).then_inc(F["qr"], 1)
                if sc_on:
                    dv.wait_ge(S["t3"], t3_ + 1)
                    dv.wait_ge(S["ohw"], t3_)
                    V.tensor_tensor(ohh[:, :, :, :], by_group(t3[:, 1, :]),
                                    hi_iota[:, :].unsqueeze(1).unsqueeze(3).broadcast_to([P, P // GRP, HI, GRP]),
                                    ALU.is_equal).then_inc(S["ohh"], 1)
                    dv.wait_ge(S["sctp"], t3_)
                    V.tensor_tensor(ohl[:, :, :], t3[:, 2, :].unsqueeze(2).broadcast_to([P, P, LO]),
                                    lo_iota[:, :].unsqueeze(1).broadcast_to([P, P, LO]),
                                    ALU.is_equal).then_inc(S["ohl"], 1)
                if att and k == 0:
                    att_sum(b)
                if att and k == 1:
                    att_smax(b)
                if list_on:
                    dv.wait_ge(S["first"], t1 + 1)
                    for l in range(HS):
                        last = V.scalar_tensor_tensor(keym[:, l, :], key[:, l, :], best[kk][:, l, 7:8],
                                                      key[:, l, :], ALU.is_lt, ALU.mult)
                        if l == HS // 2 - 1 and att and k == 0:
                            att_rsum(b)
                        if l == HS // 2 - 1 and att and k == 1:
                            att_ssum(b)
                    last.then_inc(S["mask"], 1)
                elif att and k == 0:
                    att_rsum(b)
                elif att and k == 1:
                    att_ssum(b)
                if q_on:
                    dv.wait_ge(F["sq2"], t0 + 1)
                    V.tensor_reduce(q_t2[:, :], q_sq2[:, :, :], AX, ALU.add).then_inc(F["t3"], 1)
                if att and k == 1:
                    att_probs(b)
                if pair_on:
                    dv.wait_ge(S["wfirst"], t2 + 1)
                    for h in range(H):
                        last = V.scalar_tensor_tensor(candm[:, h, :], candc[:, h, :], win[:, h, 7:8],
                                                      candc[:, h, :], ALU.is_lt, ALU.mult)
                        if h == 1 and q_on:
                            dv.wait_ge(F["t3"], t0 + 1)
                            V.tensor_scalar(q_ss2[:, :], q_t2[:, :], 1e-24, None, ALU.max).then_inc(F["ss2"], 1)
                    last.then_inc(S["wmask"], 1)
                elif q_on:
                    dv.wait_ge(F["t3"], t0 + 1)
                    V.tensor_scalar(q_ss2[:, :], q_t2[:, :], 1e-24, None, ALU.max).then_inc(F["ss2"], 1)
                if list_on:
                    dv.wait_ge(setup_v, 6)
                    dv.wait_ge(S["mask"], t1 + 1)
                    for l in range(HS):
                        last = V.max(best[kk][:, l, 8:16], keym[:, l, :])
                    last.then_inc(S["second"], 1)
                if pair_on:
                    dv.wait_ge(setup_v, 6)
                    dv.wait_ge(S["wmask"], t2 + 1)
                    for h in range(H):
                        last = V.max(win[:, h, 8:16], candm[:, h, :])
                    last.then_inc(S["wsecond"], 1)
                if att and k == 0:
                    att_token(b)
                if list_on:
                    dv.wait_ge(S["second"], t1 + 1)
                    V.tensor_scalar(
                        base[kk][:, :], best[kk][:, :, 0].bitcast(I32), -2 ** IDX, None,
                        ALU.bitwise_and).then_inc(S["base"], 1)
                if pair_on:
                    wi = win[:, :, :].bitcast(I32).rearrange("p h n -> p (h n)")
                    dv.wait_ge(S["wsecond"], t2 + 1)
                    V.tensor_scalar(valb[:, :], wi, IDX, None, ALU.logical_shift_right)
                    V.tensor_scalar(hlb[:, 0, :], wi, 4, HI - 1, ALU.logical_shift_right, ALU.bitwise_and)
                    V.tensor_scalar(hlb[:, 1, :], wi, LO - 1, None, ALU.bitwise_and).then_inc(S["dec"], 1)
                if att and k == 1:
                    att_residual(b)

            for i in range(FIRST, LOOP0):
                for k in range(2):
                    slot(i, k, stages(i, k))
            with dv.Fori(LOOP0, LOOP1) as i:
                for k in range(2):
                    slot(i, k, stages(None, k))
            for i in range(LOOP1, LAST + 1):
                for k in range(2):
                    slot(i, k, stages(i, k))

        @block.tensor
        def _(pe):
            T = nc.tensor

            def row_bias(o, row, n):
                return T.matmul(o, ones[0:1, 0:n], row, start=False, stop=True)

            pe.wait_ge(loaded, ALL_LOADED)
            pe.wait_ge(setup_v, 1)
            for h in range(H):
                T.matmul(pA[:, h * M:(h + 1) * M], wx_sb[:, h, :], wsT_sb[:, :], start=True, stop=True)
            for h in range(H):
                o = pB[0:1, h * M:(h + 1) * M]
                T.matmul(o, bxT_sb[:, h:h + 1], wsT_sb[:, :], start=True, stop=False)
                T.matmul(o, ones[0:1, 0:1], bsl_sb[:, :], start=False, stop=True)
            T.matmul(pC[0:DH, 0:DH], aq_sb[:, :], ak_sb[:, :], start=True, stop=True)
            for n in range(2):
                T.matmul(pS[0:DH, 512 * n:512 * n + 512], av_sb[:, :], wout_sb[:, 4 * n:4 * n + 4, :],
                         start=True, stop=True)
            pe.wait_ge(setup_v, 5)
            pe.wait_ge(pc, 2)
            T.transpose(pQ[:, 0:PK], k_unit[:, :, :, :].rearrange("p r s d -> p (r s d)"),
                        ident[0:PK, 0:PK]).then_inc(setup_a, 1)
            pe.wait_ge(setup_v, 6)

            def att_xT(b):
                pe.wait_ge(A["x"], b + 1)
                for k in range(TPB):
                    last = T.transpose(pA[:, k * P:(k + 1) * P], a_x[:, k, 0:D], ident[:, :])
                last.then_inc(A["xTp"], 1)

            def att_logits(b):
                pe.wait_ge(A["xT"], b + 1)
                for k in range(TPB):
                    o = pB[:, k * HM:(k + 1) * HM]
                    T.matmul(o, a_xT[:, k, :], lw[:, :], start=True, stop=False)
                    last = row_bias(o, lb[:, :], P)
                last.then_inc(A["lg"], 1)

            def att_slice(b):
                pe.wait_ge(A["sw"], b + 1)
                for c in range(CH):
                    for k in range(TPB):
                        last = T.matmul(pC[:, c * (D + 1):(c + 1) * (D + 1)], a_sw[:, k, c * P:(c + 1) * P],
                                        a_x[:, k, :], start=(k == 0), stop=(k == TPB - 1))
                last.then_inc(A["s"], 1)
                for c in range(CH):
                    for k in range(TPB):
                        last = T.transpose(pB[:, (c * TPB + k) * P:(c * TPB + k + 1) * P],
                                           a_sw[:, k, c * P:(c + 1) * P], ident[:, :])
                last.then_inc(A["swTp"], 1)

            def att_snT(b):
                pe.wait_ge(A["sn"], b + 1)
                for c in range(CH):
                    T.transpose(pA[:, c * P:(c + 1) * P], a_sn[:, c, 0:D], ident[:, :])
                    last = T.matmul(pA[0:1, 256 + c * P:256 + (c + 1) * P], a_sn[:, c, D:D + 1], ident[:, :],
                                    start=True, stop=True)
                last.then_inc(A["snTp"], 1)

            def att_st(b):
                pe.wait_ge(setup_v, 6)
                pe.wait_ge(A["snT"], b + 1)
                for h in range(H):
                    o = pC[0:DH, h * M:(h + 1) * M]
                    T.matmul(o, wfxT_sb[:, h * DH:(h + 1) * DH], a_snT[:, h * M:(h + 1) * M], start=True, stop=False)
                    last = T.matmul(o, bfx_sb[0:1, h * DH:(h + 1) * DH], a_nnT[0:1, h * M:(h + 1) * M],
                                    start=False, stop=True)
                last.then_inc(A["stp"], 1)

            def att_uv(b):
                pe.wait_ge(setup_v, 6)
                pe.wait_ge(A["stT"], b + 1)
                T.matmul(pC[0:DH, 256:512], mqk[:, :], a_stT[:, :], start=True, stop=True)
                for h in range(H):
                    c, j = divmod(h, HPC)
                    last = T.matmul(pA[32 * j:32 * j + 32, c * D:(c + 1) * D], a_stT[:, h * M:(h + 1) * M],
                                    vw[:, h, :], start=True, stop=True)
                last.then_inc(A["up"], 1)

            def att_scores(b):
                pe.wait_ge(setup_v, 6)
                pe.wait_ge(A["uT"], b + 1)
                for h in range(H):
                    c, j = divmod(h, HPC)
                    last = T.matmul(pA[32 * j:32 * j + 32, 256 + c * M:256 + (c + 1) * M],
                                    a_uT[:, h * M:(h + 1) * M], a_stT[:, h * M:(h + 1) * M], start=True, stop=True)
                last.then_inc(A["scp"], 1)

            def att_mix(b):
                pe.wait_ge(setup_v, 6)
                pe.wait_ge(A["atT"], b + 1)
                for h in range(H):
                    c, j = divmod(h, HPC)
                    last = T.matmul(pC[32 * j:32 * j + 32, c * D:(c + 1) * D], a_atT[32 * j:32 * j + 32, c, :],
                                    a_sv[32 * j:32 * j + 32, c, :], start=True, stop=True)
                last.then_inc(A["pp"], 1)

            def att_out(b):
                pe.wait_ge(A["p"], b + 1)
                for k in range(TPB):
                    o = pB[:, k * D:(k + 1) * D]
                    for c in range(CH):
                        T.matmul(o, a_swT[:, c, k * P:(k + 1) * P], a_p[:, c, :], start=(c == 0), stop=False)
                    last = row_bias(o, bout_sb[:, :], P)
                last.then_inc(A["op"], 1)

            def slot(i, k, on):
                att, q_on, _, _, sc_on, mix_on = on
                b = i + 1
                t0, t3_, t4 = 2 * i + k, 2 * i + k - 3, 2 * i + k - 4
                if mix_on:
                    pe.wait_ge(S["act"], t4 + 1)
                    T.transpose(pT[:, 384:512], act[:, :], ident[:, :]).then_inc(S["actTp"], 1)
                if q_on:
                    if k == 0:
                        pe.wait_ge(F["gate"], i)
                    pe.wait_ge(F["x2"], t0 + 1)
                    T.transpose(pM[:, 0:P], x2[k][:, :], ident[:, :]).then_inc(F["x2Tp"], 1)
                if att and k == 0:
                    att_xT(b)
                if mix_on:
                    pe.wait_ge(S["actT"], t4 + 1)
                    T.matmul(pT[:, 384:512], actT[:, :], up_sb[:, :], start=True, stop=True).then_inc(S["mix"], 1)
                if q_on:
                    pe.wait_ge(F["x2T"], t0 + 1)
                    T.matmul(pQ[:, :], x2T[k][:, :], wqc[:, :, :], start=True, stop=False)
                    row_bias(pQ[:, :], bqc[:, :, :], P)
                    pe.wait_ge(F["y"], t0)
                    T.matmul(pS[:, 0:INNER], x2T[k][:, :], wqg[:, :, :], start=True, stop=False)
                    row_bias(pS[:, 0:INNER], bqg[:, :, :], P).then_inc(F["q"], 1)
                    T.matmul(pM[:, P + k * P:2 * P + k * P], x2T[k][:, :], downT_sb[:, :],
                             start=True, stop=True).then_inc(F["inner"], 1)
                if att and k == 0:
                    att_logits(b)
                if sc_on:
                    pe.wait_ge(S["wn"], t3_ + 1)
                    pe.wait_ge(S["hl"], t3_ + 1)
                    pe.wait_ge(S["sct"], t3_)
                    pe.wait_ge(S["res"], t4 + 1 if mix_on else 0)
                    T.transpose(pT[:, 0:P], wn[:, :, :].rearrange("p h n -> p (h n)"), ident[:, :])
                    for n in range(2):
                        last = T.transpose(pT[:, (n + 1) * P:(n + 2) * P], hl[1 - k][:, n, :], ident[:, :])
                    last.then_inc(S["t3p"], 1)
                if att and k == 0:
                    att_slice(b)
                    att_snT(b) if not (q_on or sc_on) else None
                if att and k == 1:
                    att_st(b)
                    att_uv(b)
                    att_scores(b)
                if q_on:
                    pe.wait_ge(F["qn"], t0 + 1)
                    for c in range(4):
                        last = T.transpose(pQ[:, c * P:(c + 1) * P],
                                           q_n[:, 4 * c:4 * c + 4, :].rearrange("p l d -> p (l d)"), ident[:, :])
                    last.then_inc(F["qnTp"], 1)
                if sc_on:
                    pe.wait_ge(S["ohw"], t3_ + 1)
                    pe.wait_ge(S["ohl"], t3_ + 1)
                    for c in range(NG):
                        for j in range(4):
                            first = c * 4 + j
                            last = T.matmul(pT[32 * j:32 * j + 32, c * GRP * LO:(c + 1) * GRP * LO],
                                            ohw[:, first, :, :].rearrange("p h g -> p (h g)"),
                                            ohl[:, first:P:P // GRP, :], start=True, stop=True)
                    last.then_inc(S["sctp"], 1)
                if q_on:
                    pe.wait_ge(F["qnT"], t0 + 1)
                    for c in range(4):
                        last = T.matmul(pS[:, c * 256:(c + 1) * 256], q_nT[:, c, :], kb[:, :, :],
                                        start=True, stop=True)
                    last.then_inc(F["sc"], 1)
                if att and k == 0 and (q_on or sc_on):
                    att_snT(b)
                if att and k == 1:
                    att_mix(b)
                    att_out(b)

            for i in range(FIRST, LOOP0):
                for k in range(2):
                    slot(i, k, stages(i, k))
            with pe.Fori(LOOP0, LOOP1) as i:
                for k in range(2):
                    slot(i, k, stages(None, k))
            for i in range(LOOP1, LAST + 1):
                for k in range(2):
                    slot(i, k, stages(i, k))

        @block.scalar
        def _(ac):
            C = nc.scalar

            def copy(o, i_):
                return C.activation(o, i_, ACT.Copy)

            def att_xT(b):
                ac.wait_ge(A["xTp"], b + 1)
                copy(a_xT[:, :, :].rearrange("p t n -> p (t n)"), pA[:, 0:TPB * P]).then_inc(A["xT"], 1)

            def att_exp(b):
                ac.wait_ge(A["sub"], b + 1)
                C.activation(a_e[:, :, :], a_e[:, :, :], ACT.Exp).then_inc(A["exp"], 1)

            def att_swT(b):
                ac.wait_ge(A["swTp"], b + 1)
                copy(a_swT[:, :, :].rearrange("p c n -> p (c n)"), pB[:, :]).then_inc(A["swT"], 1)

            def att_snT(b):
                ac.wait_ge(A["snTp"], b + 1)
                copy(a_snT[:, :], pA[:, 0:HM])
                copy(a_nnT[:, :], pA[0:1, 256:256 + HM]).then_inc(A["snT"], 1)

            def att_stT(b):
                ac.wait_ge(A["stp"], b + 1)
                copy(a_stT[:, :], pC[0:DH, 0:HM]).then_inc(A["stT"], 1)

            def att_uT(b):
                ac.wait_ge(A["up"], b + 1)
                copy(a_uT[:, :], pC[0:DH, 256:512])
                copy(a_sv[:, :, :].rearrange("p c d -> p (c d)"), pA[:, 0:CH * D]).then_inc(A["uT"], 1)

            def att_sexp(b):
                ac.wait_ge(A["ssub"], b + 1)
                C.activation(a_se[:, :, :], a_se[:, :, :], ACT.Exp, scale=DH ** -0.5).then_inc(A["sexp"], 1)

            def att_p(b):
                ac.wait_ge(A["pp"], b + 1)
                copy(a_p[:, :, :].rearrange("p c d -> p (c d)"), pC[:, 0:CH * D]).then_inc(A["p"], 1)

            def slot(i, k, on):
                att, q_on, _, pair_on, sc_on, mix_on = on
                b = i + 1
                t0, t2, t3_, t4 = 2 * i + k, 2 * i + k - 2, 2 * i + k - 3, 2 * i + k - 4
                if mix_on:
                    ac.wait_ge(S["actTp"], t4 + 1)
                    copy(actT[:, :], pT[:, 384:512]).then_inc(S["actT"], 1)
                if q_on:
                    ac.wait_ge(F["x2Tp"], t0 + 1)
                    copy(x2T[k][:, :], pM[:, 0:P]).then_inc(F["x2T"], 1)
                if att and k == 0:
                    att_xT(b)
                if q_on:
                    ac.wait_ge(F["q"], t0 + 1)
                    C.activation(q_sq[:, :, :].rearrange("p h d -> p (h d)"), pQ[:, :], ACT.Square
                                 ).then_inc(F["sq"], 1)
                if q_on and k == 1:
                    ac.wait_ge(F["inner"], t0 + 1)
                    C.activation(gate[:, ds(t0 - 1, 2), :].rearrange("p t e -> p (t e)"), pM[:, P:3 * P],
                                 ACT.Gelu).then_inc(F["gate"], 1)
                if sc_on:
                    ac.wait_ge(S["t3p"], t3_ + 1)
                    ac.wait_ge(S["ohl"], t3_)
                    copy(t3[:, :, :].rearrange("p n t -> p (n t)"), pT[:, 0:3 * P]).then_inc(S["t3"], 1)
                if att and k == 0:
                    att_exp(b)
                if q_on:
                    ac.wait_ge(F["q1"], t0 + 1)
                    C.activation(q_sq2[:, :, :].rearrange("p l d -> p (l d)"),
                                 q_1[:, :, :].rearrange("p h d -> p (h d)"), ACT.Square).then_inc(F["sq2"], 1)
                if att and k == 0:
                    att_swT(b)
                    if not (q_on or sc_on):
                        att_snT(b)
                if att and k == 1:
                    att_stT(b)
                    att_uT(b)
                    att_sexp(b)
                if q_on:
                    ac.wait_ge(F["qnTp"], t0 + 1)
                    copy(q_nT[:, :, :].rearrange("p c t -> p (c t)"), pQ[:, :]).then_inc(F["qnT"], 1)
                if sc_on:
                    ac.wait_ge(S["sctp"], t3_ + 1)
                    ac.wait_ge(spilled, 16 * GRP * t3_)
                    copy(sct[:, :, :].rearrange("p c n -> p (c n)"), pT[:, :]).then_inc(S["sct"], 1)
                if q_on:
                    ac.wait_ge(F["sc"], t0 + 1)
                    for n in range(2):
                        last = C.activation(y[k][:, n * 512:(n + 1) * 512], pS[:, n * 512:(n + 1) * 512],
                                            ACT.Identity, bias=one_bias[:, :], scale=UNIT)
                    last.then_inc(F["y"], 1)
                if att and k == 0 and (q_on or sc_on):
                    att_snT(b)
                if pair_on:
                    ac.wait_ge(S["dec"], t2 + 1)
                    C.activation(wexp[k][:, :, :].rearrange("p h n -> p (h n)"), valb[:, :], ACT.Exp,
                                 bias=exp_bias[:, :], scale=1.0 / UNIT).then_inc(S["wexp"], 1)
                    copy(hl[k][:, :, :].rearrange("p n j -> p (n j)"),
                         hlb[:, :, :].rearrange("p n j -> p (n j)")).then_inc(S["hl"], 1)
                if att and k == 1:
                    att_p(b)

            for i in range(FIRST, LOOP0):
                for k in range(2):
                    slot(i, k, stages(i, k))
            with ac.Fori(LOOP0, LOOP1) as i:
                for k in range(2):
                    slot(i, k, stages(None, k))
            for i in range(LOOP1, LAST + 1):
                for k in range(2):
                    slot(i, k, stages(i, k))


def kernel(**inputs):
    import numpy as np
    import concourse.bacc as bacc
    from concourse import mybir as mb
    from concourse.bass_utils import run_bass_kernel_spmd

    a = {n: np.asarray(v) for n, v in inputs.items()}
    x = a["x"].astype(np.int32)
    B, N = x.shape
    D = a["L0_tok_weight"].shape[1]
    P, DH, PK = 128, a["L0_attn_Wslice"].shape[1], a["L0_ffn_keys0"].shape[0]
    arrays = [
        ("ids", x.reshape(-1, P).T), ("tok", a["L0_tok_weight"]), ("wx", a["L0_attn_Wx"]), ("wfxT", a["L0_attn_Wfx"].T),
        ("wsT", a["L0_attn_Wslice"].T), ("bxT", a["L0_attn_bx"].reshape(-1, DH).T), ("bfx", a["L0_attn_bfx"][None]),
        ("bslice", a["L0_attn_bslice"][None]), ("attn_wq", a["L0_attn_Wq"]), ("attn_wk", a["L0_attn_Wk"]),
        ("attn_wv", a["L0_attn_Wv"]), ("woutT", a["L0_attn_Wout"].T), ("bout", a["L0_attn_bout"][None]),
        ("temperature", a["L0_attn_temperature"].reshape(1, -1)), ("ffn_wqT", a["L0_ffn_Wq"].T),
        ("bq", a["L0_ffn_bq"][None]), ("ln_g", a["L0_ffn_ln_g"][None]), ("ln_b", a["L0_ffn_ln_b"][None]),
        ("keys0", a["L0_ffn_keys0"]), ("keys1", a["L0_ffn_keys1"]), ("downT", a["L0_ffn_expert_down"][:2 * PK].T),
        ("up", a["L0_ffn_expert_up"]),
    ]
    nc = bacc.Bacc("TRN2", target_bir_lowering=False, num_devices=1)
    feed, args = {}, []
    for name, v in arrays:
        v = np.ascontiguousarray(v)
        feed[name + "_dram"] = v
        args.append(nc.dram_tensor(name + "_dram", v.shape, mb.dt.from_np(v.dtype), kind="ExternalInput").ap())
    args.append(nc.dram_tensor("out_dram", (B * N, D), mb.dt.float32, kind="ExternalOutput").ap())
    tower_program(nc, *args)
    r = run_bass_kernel_spmd(nc, [feed], core_ids=[0])
    return r.results[0]["out_dram"].reshape(B, N, D)
```

```python
import concourse.bass as bass
import concourse.mybir as mybir
from contextlib import ExitStack


def tower_program(nc, ids, tok, wx, wfxT, wsT, bxT, bfx, bslice, attn_wq, attn_wk, attn_wv, woutT, bout,
                  temperature, ffn_wqT, bq, ln_g, ln_b, keys0, keys1, downT, up, out):
    F32, I32, BF16 = mybir.dt.float32, mybir.dt.int32, mybir.dt.bfloat16
    ALU, ACT, AX = mybir.AluOpType, mybir.ActivationFunctionType, mybir.AxisListType.X
    ds = bass.ds

    P = 128
    TILES = ids.shape[1]
    D = tok.shape[1]
    TPB = 2
    BATCHES = TILES // TPB
    H = temperature.shape[1]
    DH = wsT.shape[0]
    M = wsT.shape[1]
    HM = H * M
    CH = HM // P
    HPC = H // CH
    INNER = H * DH
    PK = keys0.shape[0]
    HALF = keys0.shape[1]
    K = 16
    HS = 2 * H
    E = 2 * PK
    LO = 16
    HI = E // LO
    EPS = 1e-5

    IDX = 7
    UNIT = float(2 ** 23) * 1000 / 1024
    ONE = float(2 ** 23)
    TOP = 2 ** 31 - 2 ** 24
    LEAST = 2.0 ** -126
    RECTS = [(0, 1, 0, 16), (1, 16, 0, 1), (1, 2, 1, 8), (2, 8, 1, 2), (2, 5, 2, 5)]
    NC = sum((a1 - a0) * (b1 - b0) for a0, a1, b0, b1 in RECTS)

    GRP = 4
    NG = P // GRP // 4

    BQG, BLG, BOUT = 0, INNER, INNER + HM
    ROWS = BOUT + D

    ctx = ExitStack()
    with ctx:
        def sb(name, shape, dt=F32):
            return ctx.enter_context(nc.sbuf_tensor(name, shape, dt))

        def ps(name, shape=(P, 512)):
            return ctx.enter_context(nc.psum_tensor(name, list(shape), F32))

        def sem(name):
            return ctx.enter_context(nc.semaphore(name))

        ident = sb("ident", [P, P])
        ones = sb("ones", [1, 1])
        pick = sb("pick", [96, P], BF16)
        rows = sb("rows", [1, ROWS])
        bqc_row = sb("bqc_row", [1, INNER])
        bqcT = sb("bqcT", [P, 4])
        half_c = sb("half_c", [P, 2])
        rest = sb("rest", [1, 2, ROWS])
        parts = sb("parts", [96, ROWS], BF16)
        idx_iota = sb("idx_iota", [P, PK], I32)
        lo_iota = sb("lo_iota", [P, LO, P], BF16)
        eps_c = sb("eps_c", [P, HS])
        mhalf_c = sb("mhalf_c", [P, HS])
        top_c = sb("top_c", [P, H], I32)
        one_bias = sb("one_bias", [P, 1])
        exp_bias = sb("exp_bias", [P, 1])
        warm = sb("warm", [P, 1])
        spare = sb("spare", [P, 2])
        ids_sb = sb("ids_sb", [P, TILES], I32)
        wx_sb = sb("wx_sb", [DH, H, D])
        wfxT_sb = sb("wfxT_sb", [D, INNER])
        wsT_sb = sb("wsT_sb", [DH, M])
        bxT_sb = sb("bxT_sb", [DH, H])
        bfx_sb = sb("bfx_sb", [1, INNER])
        bsl_sb = sb("bsl_sb", [1, M])
        aq_sb = sb("aq_sb", [DH, DH])
        ak_sb = sb("ak_sb", [DH, DH])
        av_sb = sb("av_sb", [DH, DH])
        wout_sb = sb("wout_sb", [DH, H, D])
        temp_sb = sb("temp_sb", [P, H])
        rtemp = sb("rtemp", [P, H])
        lw = sb("lw", [D, HM])
        mqk = sb("mqk", [DH, DH])
        vw = sb("vw", [DH, H, D])
        wqT_sb = sb("wqT_sb", [D, H, DH])
        bq_sb = sb("bq_sb", [1, H, DH])
        g_sb = sb("g_sb", [P, DH])
        b_sb = sb("b_sb", [P, DH])
        wmean = sb("wmean", [P, 2, H])
        wqc = sb("wqc", [D, H, DH])
        wqg = sb("wqg", [D, H, DH])
        k_raw = sb("k_raw", [PK, 2, HALF])
        k_sq = sb("k_sq", [PK, 2, HALF])
        k_ss = sb("k_ss", [PK, 2])
        k_rn = sb("k_rn", [PK, 2])
        k_unit = sb("k_unit", [PK, 2, 2, HALF])
        kb = sb("kb", [P, 2, PK])
        downT_sb = sb("downT_sb", [D, E])
        up_sb = sb("up_sb", [E, D])

        h_all = sb("h_all", [P, TILES, D])
        gate = sb("gate", [P, TILES, E])

        a_st = sb("a_st", [P, TILES, 6])
        a_mv = sb("a_mv", [P, TILES, 2])
        a_rs = sb("a_rs", [P, TILES])
        a_x = sb("a_x", [P, TPB, D + 1])
        a_xT = sb("a_xT", [P, TPB, P])
        a_mx = sb("a_mx", [P, TPB * H])
        a_e = sb("a_e", [P, TPB * H, M])
        a_sum = sb("a_sum", [P, TPB * H])
        a_rsum = sb("a_rsum", [P, TPB * H])
        a_sw = sb("a_sw", [P, TPB, HM])
        a_swT = sb("a_swT", [P, CH, TPB * P])
        a_den = sb("a_den", [P, CH])
        a_rden = sb("a_rden", [P, CH])
        a_sn = sb("a_sn", [P, CH, D + 1])
        a_snT = sb("a_snT", [P, HM])
        a_nnT = sb("a_nnT", [1, HM])
        a_stT = sb("a_stT", [DH, HM])
        a_uT = sb("a_uT", [DH, HM])
        a_sv = sb("a_sv", [P, CH, D])
        a_smx = sb("a_smx", [P, CH])
        a_se = sb("a_se", [P, CH, M])
        a_ssum = sb("a_ssum", [P, CH])
        a_srs = sb("a_srs", [P, CH])
        a_at = sb("a_at", [P, CH, M])
        a_atT = sb("a_atT", [P, CH, M])
        a_p = sb("a_p", [P, CH, D])

        l_st = sb("l_st", [P, TPB, 6])
        l_mv = sb("l_mv", [P, TPB, 2])
        l_rs = sb("l_rs", [P, TPB])
        x2 = [sb(f"x2_{k}", [P, D]) for k in range(2)]
        x2T = [sb(f"x2T_{k}", [P, P]) for k in range(2)]
        q_sq = sb("q_sq", [P, 4, P])
        q_ss = sb("q_ss", [P, H])
        q_rs = sb("q_rs", [P, H])
        q_r = sb("q_r", [P, H, DH])
        q_1 = sb("q_1", [P, H, DH])
        q_sq2 = sb("q_sq2", [P, HS, HALF])
        q_ss2 = sb("q_ss2", [P, HS])
        q_t2 = sb("q_t2", [P, HS])
        q_rn = sb("q_rn", [P, HS])
        q_n = sb("q_n", [P, HS, HALF])
        q_nT = sb("q_nT", [P, 4, P])
        y = [sb(f"y{k}", [P, HS * PK], I32) for k in range(2)]

        key = sb("key", [P, HS, PK])
        keylt = sb("keylt", [P, HS, PK])
        keym = sb("keym", [P, HS, PK])
        best = [sb(f"best{k}", [P, HS, K]) for k in range(2)]
        base = [sb(f"base{k}", [P, HS], I32) for k in range(2)]
        based = sb("based", [P, H], I32)
        rel = sb("rel", [P, HS, K], I32)
        cand = sb("cand", [P, H, NC], I32)
        candc = sb("candc", [P, H, NC])
        candlt = sb("candlt", [P, H, NC])
        candm = sb("candm", [P, H, NC])
        win = sb("win", [P, H, K])
        valb = sb("valb", [P, H * K], I32)
        hlb = sb("hlb", [P, 2, H * K], I32)
        wexp = [sb(f"wexp{k}", [P, H, K]) for k in range(2)]
        hl = [sb(f"hl{k}", [P, 2, H * K]) for k in range(2)]
        wsum = sb("wsum", [P, H])
        wrec = sb("wrec", [P, H])
        wn = sb("wn", [P, H, K])
        t3 = sb("t3", [P, 2, P])
        lo_t = sb("lo_t", [P, P], BF16)
        ohlb = sb("ohlb", [P, LO, P], BF16)
        ohl = sb("ohl", [P, LO, P])
        ohw = sb("ohw", [P, P // GRP, HI, GRP])
        sct = sb("sct", [P, NG, GRP * LO])
        wacc = [sb(f"wacc{k}", [P, E]) for k in range(2)]
        act = sb("act", [P, E])
        actT = sb("actT", [P, P])
        res = [sb(f"res{k}", [P, D]) for k in range(2)]

        pA, pB, pC = ps("pA"), ps("pB"), ps("pC")
        pM = ps("pM")
        pQ = ps("pQ")
        pS = ps("pS", [P, 1024])
        pT = ps("pT")

        loaded = sem("loaded"); ids_in = sem("ids_in"); gathered0 = sem("gathered0"); gathered = sem("gathered")
        pc = sem("pc"); setup_v = sem("setup_v"); setup_p = sem("setup_p"); setup_t = sem("setup_t")
        setup_a = sem("setup_a"); setup_b = sem("setup_b")
        A = {n: sem("a_" + n + "_done") for n in (
            "st", "mv", "t", "rs", "x", "xTp", "xT", "lg", "mx", "sub", "exp", "sum", "rsum", "sw", "s", "swTp", "swT",
            "den", "rden", "sn", "snTp", "snT", "stp", "stT", "up", "uT", "scp", "smx", "ssub", "sexp", "ssum",
            "srs", "at", "atT", "pp", "p", "op", "h2")}
        F = {n: sem("f_" + n + "_done") for n in (
            "st", "mv", "t", "rs", "x2", "x2Tp", "x2T", "qc", "q", "inner", "ssp", "sq", "gate", "ss", "t2", "rq", "qr", "q1",
            "sq2", "ss2", "t3", "rn", "qn", "qnTp", "qnT", "sc", "y")}
        S = {n: sem("s_" + n + "_done") for n in (
            "key", "first", "lt", "mask", "second", "base", "based", "rel", "cand", "clamp", "wfirst", "wlt", "wmask", "wsecond",
            "dec", "wexp", "hl", "wsum", "wrec", "wn", "t3p", "t3", "ohlb", "ohl", "ohw", "sctp", "sct",
            "act", "actTp", "actT", "mix", "res")}
        spilled = sem("spilled")
        wacc_in = [sem(f"wacc_in{k}") for k in range(2)]
        stored = [sem(f"stored{k}") for k in range(2)]

        LOADS = [(wx_sb[:, :, :], wx.rearrange("(h d) i -> d h i", d=DH)), (wsT_sb[:, :], wsT), (bxT_sb[:, :], bxT),
                 (bsl_sb[:, :], bslice), (temp_sb[:, :], temperature.partition_broadcast(P)),
                 (aq_sb[:, :], attn_wq), (ak_sb[:, :], attn_wk), (av_sb[:, :], attn_wv),
                 (wout_sb[:, :, :], woutT.rearrange("(h i) o -> i h o", i=DH)), (wfxT_sb[:, :], wfxT),
                 (bfx_sb[:, :], bfx), (rows[:, BOUT:ROWS], bout),
                 (wqT_sb[:, :, :], ffn_wqT.rearrange("p (h d) -> p h d", d=DH)),
                 (bq_sb[:, :, :], bq.rearrange("p (h d) -> p h d", d=DH)),
                 (g_sb[:, :], ln_g.partition_broadcast(P)), (b_sb[:, :], ln_b.partition_broadcast(P)),
                 (k_raw[:, 0, :], keys0), (k_raw[:, 1, :], keys1), (downT_sb[:, :], downT), (up_sb[:, :], up[0:E, :])]
        ALL_LOADED = 16 * len(LOADS)

        FIRST, LAST = -1, BATCHES + 2
        LOOP0, LOOP1 = 3, BATCHES - 1

        def by_group(row):
            return row.rearrange("p (g n) -> p n g", g=GRP)

        def stages(i, k):
            if i is None:
                return (True,) * 8
            t = [2 * i + k - n for n in range(6)]
            return (i + 1 < BATCHES, *[0 <= x < TILES for x in t], 0 <= t[0] + 1 < TILES)

        scratch = [nc.dram_tensor(f"scratch{k}", [P, E], F32, kind="Internal").ap() for k in range(2)]
        block = ctx.enter_context(nc.Block())

        @block.sync
        def _(sp):
            sp.dma_start(ids_sb[:, :], ids).then_inc(ids_in, 16)
            for dst, src in LOADS:
                sp.dma_start(dst, src).then_inc(loaded, 16)

            def slot(i, k, on):
                sc_on, mix_on = on[5:7]
                t4, t5 = 2 * i + k - 4, 2 * i + k - 5
                if sc_on:
                    sp.wait_ge(S["sct"], t4 + 1)
                    for g in range(GRP):
                        sp.dma_start(
                            scratch[k].rearrange("(g c j) (h l) -> g (j h) c l", g=GRP, c=NG, l=LO)[g],
                            sct[g:P:GRP, :, g * LO:(g + 1) * LO]).then_inc(spilled, 16)
                if mix_on:
                    sp.wait_ge(S["res"], t5 + 1)
                    sp.dma_start(out[ds(t5 * P, P), :], res[1 - k][:, :]).then_inc(stored[1 - k], 16)
                if sc_on:
                    sp.wait_ge(spilled, 16 * GRP * (t4 + 1))
                    if mix_on:
                        sp.wait_ge(S["act"], t5)
                    sp.dma_start(wacc[k][:, :], scratch[k]).then_inc(wacc_in[k], 16)

            for i in range(FIRST, LOOP0):
                for k in range(2):
                    slot(i, k, stages(i, k))
            with sp.Fori(LOOP0, LOOP1) as i:
                for k in range(2):
                    slot(i, k, stages(None, k))
            for i in range(LOOP1, LAST + 1):
                for k in range(2):
                    slot(i, k, stages(i, k))
            for k in range(2):
                sp.wait_ge(stored[k], 16 * (TILES // 2))

        @block.gpsimd
        def _(gp):
            G = nc.gpsimd
            G.memset(ident[:, :], 0.0).then_inc(pc, 1)
            gp.wait_ge(pc, 1)
            G.affine_select(out=ident[:, :], in_=ident[:, :], compare_op=ALU.not_equal, fill=1.0, base=0,
                            pattern=[[-1, P]], channel_multiplier=1).then_inc(pc, 1)
            gp.wait_ge(ids_in, 16)
            for t in range(TILES):
                G.indirect_dma_start(h_all[:, t, :], None, tok[:, :],
                                     bass.IndirectOffsetOnAxis(ap=ids_sb[:, t:t + 1], axis=0)).then_inc(
                                         gathered0 if t < TPB else gathered, 16)
                if t == TPB - 1:
                    G.iota(idx_iota[:, :], [[1, PK]], 0, 0)
                    G.iota(lo_iota[:, :, :], [[1, LO], [0, P]], 0, 0, allow_small_or_imprecise_dtypes=True)
                    G.memset(top_c[:, :], TOP)
                    G.memset(eps_c[:, :], EPS)
                    G.memset(mhalf_c[:, :], -0.5).then_inc(pc, 1)
                    gp.wait_ge(pc, 3)
                    gp.wait_ge(setup_v, 1)
                    G.tensor_tensor(k_rn[:, :], k_ss[:, :], mhalf_c[0:PK, 0:2], ALU.pow).then_inc(setup_p, 1)

            def candidates(k, tl):
                bs = base[k][:, :].rearrange("p (h s) -> p h s", s=2)
                bt = best[k][:, :, :].bitcast(I32).rearrange("p (h s) n -> p h s n", s=2)
                rl = rel[:, :, :].rearrange("p (h s) n -> p h s n", s=2)
                gp.wait_ge(S["base"], tl + 1)
                G.tensor_tensor(based[:, :], bs[:, :, 1], top_c[:, :], ALU.subtract).then_inc(S["based"], 1)
                G.tensor_tensor(rl[:, :, 0, :], bt[:, :, 0, :],
                                bs[:, :, 0:1].broadcast_to([P, H, K]), ALU.subtract)
                gp.wait_ge(S["based"], tl + 1)
                G.tensor_tensor(rl[:, :, 1, :], bt[:, :, 1, :],
                                based[:, :].unsqueeze(2).broadcast_to([P, H, K]), ALU.subtract
                                ).then_inc(S["rel"], 1)
                gp.wait_ge(S["rel"], tl + 1)
                gp.wait_ge(S["clamp"], tl)
                at = 0
                for n, (a0, a1, b0, b1) in enumerate(RECTS):
                    na, nb = a1 - a0, b1 - b0
                    o = cand[:, :, at:at + na * nb].rearrange("p h (a b) -> p h a b", b=nb)
                    ins = G.tensor_tensor(
                        o, rl[:, :, 0, a0:a1].unsqueeze(3).broadcast_to([P, H, na, nb]),
                        rl[:, :, 1, b0:b1].unsqueeze(2).broadcast_to([P, H, na, nb]), ALU.add)
                    at += na * nb
                ins.then_inc(S["cand"], 1)

            def att_deviation(n, tiles):
                gp.wait_ge(A["mv"], n)
                G.tensor_tensor(a_rs[:, tiles], a_mv[:, tiles, 1], eps_c[:, tiles], ALU.add).then_inc(A["t"], 1)
                gp.wait_ge(A["t"], n)
                G.tensor_tensor(a_rs[:, tiles], a_rs[:, tiles], mhalf_c[:, tiles], ALU.pow).then_inc(A["rs"], 1)

            def deviation(t0):
                gp.wait_ge(F["ss"], t0 + 1)
                G.tensor_tensor(q_rs[:, :], q_ss[:, :], mhalf_c[:, 0:H], ALU.pow).then_inc(F["rq"], 1)

            def unit_halves(t0):
                gp.wait_ge(F["ss2"], t0 + 1)
                G.tensor_tensor(q_rn[:, :], q_ss2[:, :], mhalf_c[:, :], ALU.pow).then_inc(F["rn"], 1)
                gp.wait_ge(F["rn"], t0 + 1)
                G.tensor_tensor(q_n[:, :, :], q_1[:, :, :].rearrange("p h (s d) -> p (h s) d", d=HALF),
                                q_rn[:, :].unsqueeze(2).broadcast_to([P, HS, HALF]),
                                ALU.mult).then_inc(F["qn"], 1)

            def slot(i, k, on):
                att, q_on, _, list_on, pair_on, sc_on, mix_on, _ = on
                b, kk = i + 1, 1 - k
                t0, _, tl, tp, ts, tm = (2 * i + k - n for n in range(6))
                if list_on:
                    gp.wait_ge(S["lt"], tl + 1)
                    gp.wait_ge(S["second"], tl)
                    G.tensor_tensor(keym[:, :, :], key[:, :, :], keylt[:, :, :], ALU.mult).then_inc(S["mask"], 1)
                if q_on:
                    deviation(t0)
                if q_on:
                    gp.wait_ge(F["qr"], t0 + 1)
                    G.tensor_tensor(q_1[:, :, :], q_r[:, :, :], b_sb[:, :].unsqueeze(1).broadcast_to([P, H, DH]),
                                    ALU.add).then_inc(F["q1"], 1)
                if mix_on:
                    gp.wait_ge(wacc_in[kk], 16 * (i - 2 + k))
                    gp.wait_ge(F["gate"], i - 2 + k)
                    gp.wait_ge(S["actTp"], tm)
                    G.tensor_tensor(act[:, :], wacc[kk][:, :], gate[:, ds(tm, 1), :], ALU.mult).then_inc(S["act"], 1)
                if att and k == 0:
                    gp.wait_ge(A["rsum"], b + 1)
                    G.tensor_tensor(a_sw[:, :, :].rearrange("p t (h m) -> p (t h) m", m=M), a_e[:, :, :],
                                    a_rsum[:, :].unsqueeze(2).broadcast_to([P, TPB * H, M]),
                                    ALU.mult).then_inc(A["sw"], 1)
                if list_on and k == 1:
                    candidates(k, tl)
                if q_on and k == 1:
                    unit_halves(t0)
                if list_on and k == 0:
                    candidates(k, tl)
                if q_on and k == 0:
                    unit_halves(t0)
                if att and k == 1:
                    gp.wait_ge(F["mv"], b + 1)
                    G.tensor_tensor(l_rs[:, :], l_mv[:, :, 1], eps_c[:, 0:TPB], ALU.add).then_inc(F["t"], 1)
                    gp.wait_ge(F["t"], b + 1)
                    G.tensor_tensor(l_rs[:, :], l_rs[:, :], mhalf_c[:, 0:TPB], ALU.pow).then_inc(F["rs"], 1)
                if pair_on:
                    gp.wait_ge(S["wrec"], tp + 1)
                    gp.wait_ge(S["wexp"], tp + 1)
                    gp.wait_ge(S["t3p"], tp)
                    G.tensor_tensor(wn[:, :, :], wexp[kk][:, :, :],
                                    wrec[:, :].unsqueeze(2).broadcast_to([P, H, K]), ALU.mult).then_inc(S["wn"], 1)
                if list_on:
                    gp.wait_ge(S["wlt"], tl + 1)
                    gp.wait_ge(S["wsecond"], tl)
                    G.tensor_tensor(candm[:, :, :], candc[:, :, :], candlt[:, :, :], ALU.mult).then_inc(S["wmask"], 1)

            att_deviation(1, slice(0, TPB))
            for i in range(FIRST, LOOP0):
                for k in range(2):
                    slot(i, k, stages(i, k))
                    if i == FIRST and k == 0:
                        att_deviation(2, slice(TPB, TILES))
            with gp.Fori(LOOP0, LOOP1) as i:
                for k in range(2):
                    slot(i, k, stages(None, k))
            for i in range(LOOP1, LAST + 1):
                for k in range(2):
                    slot(i, k, stages(i, k))

        @block.vector
        def _(dv):
            V = nc.vector
            bqc = bqc_row[:, :].rearrange("p (h d) -> p h d", d=DH)
            bqg = rows[:, BQG:BQG + INNER].rearrange("p (h d) -> p h d", d=DH)
            brow = rows[:, BLG:BLG + HM].rearrange("p (h m) -> p h m", m=M)
            V.memset(ones[:, :], 1.0)
            V.memset(pick[:, :], 0.0)
            V.memset(parts[:, :], 0.0)
            V.memset(kb[:, :, :], 0.0)
            for h in range(2):
                V.memset(half_c[h * DH:(h + 1) * DH, h:h + 1], 1.0 / DH)
                V.memset(half_c[h * DH:(h + 1) * DH, 1 - h:2 - h], 0.0)
            V.memset(one_bias[:, :], ONE)
            V.memset(exp_bias[:, :], -float(TOP >> IDX) / UNIT)
            for k in range(TPB):
                V.memset(a_x[:, k, D:D + 1], 1.0)
            dv.wait_ge(loaded, ALL_LOADED)
            V.tensor_tensor(k_sq[:, :, :], k_raw[:, :, :], k_raw[:, :, :], ALU.mult).then_inc(setup_t, 1)
            dv.wait_ge(setup_t, 1)
            V.tensor_reduce(k_rn[:, :], k_sq[:, :, :], AX, ALU.add).then_inc(setup_t, 1)
            dv.wait_ge(setup_t, 2)
            V.tensor_scalar(k_ss[:, :], k_rn[:, :], 1e-24, None, ALU.max).then_inc(setup_v, 1)
            V.reciprocal(rtemp[:, :], temp_sb[:, :])
            V.tensor_reduce(wmean[:, 0, :], wqT_sb[:, :, :], AX, ALU.add)
            V.tensor_reduce(wmean[0:1, 1, :], bq_sb[:, :, :], AX, ALU.add).then_inc(setup_t, 1)
            dv.wait_ge(setup_t, 3)
            V.tensor_scalar(wmean[:, 0, :], wmean[:, 0, :], 1.0 / DH, None, ALU.mult)
            V.tensor_scalar(wmean[0:1, 1, :], wmean[0:1, 1, :], 1.0 / DH, None, ALU.mult).then_inc(setup_t, 1)
            dv.wait_ge(setup_t, 4)
            V.tensor_tensor(wqc[:, :, :], wqT_sb[:, :, :], wmean[:, 0, :].unsqueeze(2).broadcast_to([D, H, DH]),
                            ALU.subtract)
            V.tensor_tensor(bqc, bq_sb[:, :, :], wmean[0:1, 1, :].unsqueeze(2).broadcast_to([1, H, DH]),
                            ALU.subtract).then_inc(setup_t, 1)
            dv.wait_ge(setup_t, 5)
            V.tensor_tensor(wqg[:, :, :], wqc[:, :, :], g_sb[:, :].unsqueeze(1).broadcast_to([D, H, DH]), ALU.mult)
            V.tensor_tensor(bqg, bqc, g_sb[0:1, :].unsqueeze(1).broadcast_to([1, H, DH]),
                            ALU.mult)
            dv.wait_ge(setup_p, 1)
            for s in range(2):
                for r in range(2):
                    V.tensor_scalar(k_unit[:, r, s, :], k_raw[:, s, :], k_rn[:, s:s + 1], None,
                                    ALU.mult).then_inc(setup_v, 1)
            dv.wait_ge(setup_a, 1)
            V.tensor_tensor(lw[:, :].rearrange("p (h m) -> p h m", m=M),
                            pA[:, 0:HM].rearrange("p (h m) -> p h m", m=M),
                            rtemp[:, :].unsqueeze(2).broadcast_to([D, H, M]), ALU.mult)
            V.tensor_tensor(brow,
                            pB[0:1, 0:HM].rearrange("p (h m) -> p h m", m=M),
                            rtemp[0:1, :].unsqueeze(2).broadcast_to([1, H, M]), ALU.mult).then_inc(setup_t, 1)
            dv.wait_ge(setup_t, 6)
            for n in range(3):
                V.memset(pick[32 * n:32 * n + 1, :], 1.0)
                left = rows[:, :] if n == 0 else rest[:, n - 1, :]
                V.tensor_copy(parts[32 * n:32 * n + 1, :], left).then_inc(setup_t, 1)
                if n < 2:
                    dv.wait_ge(setup_t, 7 + 2 * n)
                    V.tensor_tensor(rest[:, n, :], left, parts[32 * n:32 * n + 1, :],
                                    ALU.subtract).then_inc(setup_t, 1)
                    dv.wait_ge(setup_t, 8 + 2 * n)
            V.tensor_copy(mqk[:, :], pC[0:DH, 0:DH])
            for n in range(2):
                V.tensor_copy(vw[:, 4 * n:4 * n + 4, :], pS[0:DH, 512 * n:512 * n + 512].rearrange(
                    "p (h o) -> p h o", o=D))
            for n in range(4):
                last = V.tensor_copy(kb[32 * n:32 * n + 32, n % 2, :], pQ[32 * n:32 * n + 32, 0:PK])
            last.then_inc(setup_v, 1)

            def att_stats(n, tiles, arrived, count):
                dv.wait_ge(arrived, count)
                for t in tiles:
                    last = V.bn_stats(a_st[:, t, :], h_all[:, t, :])
                last.then_inc(A["st"], 1)
                dv.wait_ge(A["st"], n)
                for t in tiles:
                    last = V.bn_aggr(a_mv[:, t, :], a_st[:, t, :])
                last.then_inc(A["mv"], 1)

            def att_norm(b):
                dv.wait_ge(A["rs"], 1 if isinstance(b, int) and b == 0 else 2)
                for k in range(TPB):
                    t = b * TPB + k
                    last = V.tensor_scalar(a_x[:, k, 0:D], h_all[:, ds(t, 1), :].squeeze(1), a_mv[:, ds(t, 1), 0:1].squeeze(1),
                                           a_rs[:, ds(t, 1)], ALU.subtract, ALU.mult)
                last.then_inc(A["x"], 1)

            lg = pB[:, :].rearrange("p (g m) -> p g m", m=M)

            def att_max(b):
                dv.wait_ge(A["lg"], b + 1)
                V.tensor_reduce(a_mx[:, :], lg, AX, ALU.max).then_inc(A["mx"], 1)

            def att_sub(b):
                dv.wait_ge(A["mx"], b + 1)
                V.tensor_tensor(a_e[:, :, :], lg, a_mx[:, :].unsqueeze(2).broadcast_to([P, TPB * H, M]),
                                ALU.subtract).then_inc(A["sub"], 1)

            def att_sum(b):
                dv.wait_ge(A["exp"], b + 1)
                V.tensor_reduce(a_sum[:, :], a_e[:, :, :], AX, ALU.add).then_inc(A["sum"], 1)

            def att_rsum(b):
                dv.wait_ge(A["sum"], b + 1)
                V.reciprocal(a_rsum[:, :], a_sum[:, :]).then_inc(A["rsum"], 1)

            sl = pC[:, 0:CH * (D + 1)].rearrange("p (c d) -> p c d", d=D + 1)

            def att_token(b):
                dv.wait_ge(A["s"], b + 1)
                V.tensor_scalar(a_den[:, :], sl[:, :, D], EPS, None, ALU.add).then_inc(A["den"], 1)
                dv.wait_ge(A["den"], b + 1)
                V.reciprocal(a_rden[:, :], a_den[:, :]).then_inc(A["rden"], 1)
                dv.wait_ge(A["rden"], b + 1)
                V.tensor_tensor(a_sn[:, :, :], sl, a_rden[:, :].unsqueeze(2).broadcast_to([P, CH, D + 1]),
                                ALU.mult).then_inc(A["sn"], 1)

            scp = pA[:, 256:256 + CH * M].rearrange("p (c m) -> p c m", m=M)

            def att_smax(b):
                dv.wait_ge(A["scp"], b + 1)
                V.tensor_reduce(a_smx[:, :], scp, AX, ALU.max).then_inc(A["smx"], 1)
                dv.wait_ge(A["smx"], b + 1)
                V.tensor_tensor(a_se[:, :, :], scp, a_smx[:, :].unsqueeze(2).broadcast_to([P, CH, M]),
                                ALU.subtract).then_inc(A["ssub"], 1)

            def att_ssum(b):
                dv.wait_ge(A["sexp"], b + 1)
                V.tensor_reduce(a_ssum[:, :], a_se[:, :, :], AX, ALU.add).then_inc(A["ssum"], 1)
                dv.wait_ge(A["ssum"], b + 1)
                V.reciprocal(a_srs[:, :], a_ssum[:, :]).then_inc(A["srs"], 1)

            def att_probs(b):
                dv.wait_ge(A["srs"], b + 1)
                V.tensor_tensor(a_at[:, :, :], a_se[:, :, :], a_srs[:, :].unsqueeze(2).broadcast_to([P, CH, M]),
                                ALU.mult).then_inc(A["at"], 1)
                dv.wait_ge(A["at"], b + 1)
                V.transpose(a_atT[:, :, :].rearrange("p c m -> p (c m)"),
                            a_at[:, :, :].rearrange("p c m -> p (c m)")).then_inc(A["atT"], 1)

            def att_residual(b):
                dv.wait_ge(A["op"], b + 1)
                hb = h_all[:, ds(b * TPB, TPB), :]
                V.tensor_tensor(hb, pB[:, 0:TPB * D].rearrange("p (t d) -> p t d", d=D), hb,
                                ALU.add).then_inc(A["h2"], 1)

            def first_eight(k, l0, l1):
                for l in range(l0, l1):
                    last = V.max(best[k][:, l, 0:8], key[:, l, :])
                return last

            def next_eight(k, l0, l1):
                for l in range(l0, l1):
                    last = V.max(best[k][:, l, 8:16], keym[:, l, :])
                return last

            def below(o, keys, eighth):
                return V.tensor_tensor(o, keys, eighth.broadcast_to(keys.shape), ALU.is_lt)

            def query_stats(b):
                dv.wait_ge(A["h2"], b + 1)
                V.memset(spare[:, 1:2], 0.0)
                for n in range(TPB):
                    last = V.bn_stats(l_st[:, n, :], h_all[:, ds(b * TPB + n, 1), :])
                last.then_inc(F["st"], 1)
                dv.wait_ge(F["st"], b + 1)
                V.memset(spare[:, 1:2], 0.0)
                for n in range(TPB):
                    last = V.bn_aggr(l_mv[:, n, :], l_st[:, n, :])
                last.then_inc(F["mv"], 1)

            def first_pairs(tl):
                dv.wait_ge(S["cand"], tl + 1)
                V.tensor_scalar(candc[:, :, :], cand[:, :, :].bitcast(F32), LEAST, None,
                                ALU.max).then_inc(S["clamp"], 1)
                dv.wait_ge(setup_v, 6)
                dv.wait_ge(S["clamp"], tl + 1)
                for h in range(H):
                    last = V.max(win[:, h, 0:8], candc[:, h, :])
                last.then_inc(S["wfirst"], 1)
                dv.wait_ge(S["wfirst"], tl + 1)
                dv.wait_ge(S["wmask"], tl)
                below(candlt[:, :, :], candc[:, :, :], win[:, :, 7:8]).then_inc(S["wlt"], 1)

            def query_squares(t0):
                dv.wait_ge(F["ssp"], t0 + 1)
                V.tensor_scalar(q_ss[:, :], pT[:, 384:384 + H], EPS, None, ALU.add).then_inc(F["ss"], 1)

            def half_squares(t0):
                dv.wait_ge(F["sq2"], t0 + 1)
                V.tensor_reduce(q_t2[:, :], q_sq2[:, :, :], AX, ALU.add).then_inc(F["t3"], 1)
                dv.wait_ge(F["t3"], t0 + 1)
                V.tensor_scalar(q_ss2[:, :], q_t2[:, :], 1e-24, None, ALU.max).then_inc(F["ss2"], 1)

            def result(kk, tm, before):
                dv.wait_ge(S["mix"], tm + 1)
                dv.wait_ge(stored[kk], 16 * before)
                V.tensor_tensor(res[kk][:, :], pA[:, 384:512], h_all[:, ds(tm, 1), :].squeeze(1),
                                ALU.add).then_inc(S["res"], 1)

            def slot(i, k, on):
                att, q_on, late_on, list_on, pair_on, sc_on, mix_on, next_on = on
                b, kk = i + 1, 1 - k
                t0, t1, tl, tp, ts, tm = (2 * i + k - n for n in range(6))
                if list_on:
                    dv.wait_ge(S["key"], tl + 1)
                    V.memset(spare[:, 0:1], 0.0)
                if list_on:
                    first_eight(k, 0, HS).then_inc(S["first"], 1)
                if att and k == 0:
                    att_norm(b)
                if list_on:
                    dv.wait_ge(S["first"], tl + 1)
                    dv.wait_ge(S["mask"], tl)
                    below(keylt[:, :, :], key[:, :, :], best[k][:, :, 7:8]).then_inc(S["lt"], 1)
                if q_on:
                    query_squares(t0)
                if sc_on:
                    dv.wait_ge(S["t3"], ts + 1)
                    dv.wait_ge(S["sctp"], ts)
                    dv.wait_ge(S["ohl"], ts)
                    V.tensor_tensor(ohlb[:, :, :], lo_t[:, :].unsqueeze(1).broadcast_to([P, LO, P]),
                                    lo_iota[:, :, :], ALU.is_equal).then_inc(S["ohlb"], 1)
                    for n in range(HI):
                        last = V.scalar_tensor_tensor(ohw[:, :, n, :], by_group(t3[:, 1, :]), float(n),
                                                      by_group(t3[:, 0, :]), ALU.is_equal, ALU.mult)
                    last.then_inc(S["ohw"], 1)
                if att and k == 0:
                    att_max(b)
                if list_on:
                    dv.wait_ge(setup_v, 6)
                    dv.wait_ge(S["mask"], tl + 1)
                    next_eight(k, 0, HS // 2)
                if att and k == 0:
                    att_sub(b)
                if q_on:
                    dv.wait_ge(F["rq"], t0 + 1)
                    dv.wait_ge(F["q"], t0 + 1)
                    V.tensor_tensor(q_r[:, :, :], pS[:, 0:INNER].rearrange("p (h d) -> p h d", d=DH),
                                    q_rs[:, :].unsqueeze(2).broadcast_to([P, H, DH]), ALU.mult).then_inc(F["qr"], 1)
                if list_on:
                    next_eight(k, HS // 2, HS).then_inc(S["second"], 1)
                if att and k == 0:
                    att_sum(b)
                    att_rsum(b)
                if att and k == 1:
                    att_smax(b)
                if list_on:
                    dv.wait_ge(S["second"], tl + 1)
                    V.tensor_scalar(base[k][:, :], best[k][:, :, 0].bitcast(I32), -2 ** IDX, None,
                                    ALU.bitwise_and).then_inc(S["base"], 1)
                if q_on:
                    half_squares(t0)
                if att and k == 1:
                    att_ssum(b)
                if pair_on:
                    dv.wait_ge(setup_v, 6)
                    dv.wait_ge(S["wmask"], tp + 1)
                    for h in range(H):
                        last = V.max(win[:, h, 8:16], candm[:, h, :])
                    last.then_inc(S["wsecond"], 1)
                if att and k == 1:
                    att_probs(b)
                if pair_on:
                    wi = win[:, :, :].bitcast(I32).rearrange("p h n -> p (h n)")
                    dv.wait_ge(S["wsecond"], tp + 1)
                    V.tensor_scalar(valb[:, :], wi, IDX, None, ALU.logical_shift_right)
                    V.tensor_scalar(hlb[:, 0, :], wi, 4, HI - 1, ALU.logical_shift_right, ALU.bitwise_and)
                    V.tensor_scalar(hlb[:, 1, :], wi, LO - 1, None, ALU.bitwise_and).then_inc(S["dec"], 1)
                if late_on:
                    dv.wait_ge(F["y"], t1 + 1)
                    V.scalar_tensor_tensor(key[:, :, :].bitcast(I32), y[kk][:, :].rearrange("p (l e) -> p l e", e=PK),
                                           IDX, idx_iota[:, :].unsqueeze(1).broadcast_to([P, HS, PK]),
                                           ALU.logical_shift_left, ALU.bitwise_or).then_inc(S["key"], 1)
                if list_on and k == 1:
                    first_pairs(tl)
                if att and k == 1:
                    att_residual(b)
                    query_stats(b)
                if pair_on:
                    dv.wait_ge(S["wexp"], tp + 1)
                    V.tensor_reduce(wsum[:, :], wexp[kk][:, :, :], AX, ALU.add).then_inc(S["wsum"], 1)
                if pair_on:
                    dv.wait_ge(S["wsum"], tp + 1)
                    V.reciprocal(wrec[:, :], wsum[:, :]).then_inc(S["wrec"], 1)
                if att and k == 0:
                    att_token(b)
                if mix_on and k == 0:
                    result(kk, tm, i - 3 + k)
                if mix_on and k == 1:
                    result(kk, tm, i - 3 + k)
                if next_on:
                    dv.wait_ge(F["rs"], i + 1 + k)
                    V.tensor_scalar(x2[kk][:, :], h_all[:, ds(t0 + 1, 1), :].squeeze(1), l_mv[:, kk, 0:1],
                                    l_rs[:, kk:kk + 1], ALU.subtract, ALU.mult).then_inc(F["x2"], 1)
                if list_on and k == 0:
                    first_pairs(tl)

            att_stats(1, range(TPB), gathered0, 16 * TPB)

            for i in range(FIRST, LOOP0):
                for k in range(2):
                    slot(i, k, stages(i, k))
                    if i == FIRST and k == 0:
                        att_stats(2, range(TPB, TILES), gathered, 16 * (TILES - TPB))
            with dv.Fori(LOOP0, LOOP1) as i:
                for k in range(2):
                    slot(i, k, stages(None, k))
            for i in range(LOOP1, LAST + 1):
                for k in range(2):
                    slot(i, k, stages(i, k))

        @block.tensor
        def _(pe):
            T = nc.tensor

            def row_bias(o, at, n):
                return T.matmul(o, pick[:, :], parts[:, at:at + n], start=False, stop=True)

            pe.wait_ge(loaded, ALL_LOADED)
            pe.wait_ge(setup_v, 1)
            for h in range(H):
                T.matmul(pA[:, h * M:(h + 1) * M], wx_sb[:, h, :], wsT_sb[:, :], start=True, stop=True)
            for h in range(H):
                o = pB[0:1, h * M:(h + 1) * M]
                T.matmul(o, bxT_sb[:, h:h + 1], wsT_sb[:, :], start=True, stop=False)
                T.matmul(o, ones[0:1, 0:1], bsl_sb[:, :], start=False, stop=True)
            T.matmul(pC[0:DH, 0:DH], aq_sb[:, :], ak_sb[:, :], start=True, stop=True)
            for n in range(2):
                T.matmul(pS[0:DH, 512 * n:512 * n + 512], av_sb[:, :], wout_sb[:, 4 * n:4 * n + 4, :],
                         start=True, stop=True)
            pe.wait_ge(setup_v, 5)
            pe.wait_ge(pc, 2)
            T.transpose(pQ[:, 0:PK], k_unit[:, :, :, :].rearrange("p r s d -> p (r s d)"),
                        ident[0:PK, 0:PK]).then_inc(setup_a, 1)
            for c in range(4):
                last = T.matmul(pM[:, c:c + 1], bqc_row[:, c * P:(c + 1) * P], ones[0:1, 0:1], start=True, stop=True)
            last.then_inc(setup_a, 1)
            pe.wait_ge(setup_v, 6)
            pe.wait_ge(setup_b, 1)

            def att_xT(b):
                pe.wait_ge(A["x"], b + 1)
                for k in range(TPB):
                    last = T.transpose(pA[:, k * P:(k + 1) * P], a_x[:, k, 0:D], ident[:, :])
                last.then_inc(A["xTp"], 1)

            def att_logits(b):
                pe.wait_ge(A["xT"], b + 1)
                for k in range(TPB):
                    o = pB[:, k * HM:(k + 1) * HM]
                    T.matmul(o, a_xT[:, k, :], lw[:, :], start=True, stop=False)
                    last = row_bias(o, BLG, HM)
                last.then_inc(A["lg"], 1)

            def att_slice(b):
                pe.wait_ge(A["sw"], b + 1)
                for c in range(CH):
                    for k in range(TPB):
                        last = T.matmul(pC[:, c * (D + 1):(c + 1) * (D + 1)], a_sw[:, k, c * P:(c + 1) * P],
                                        a_x[:, k, :], start=(k == 0), stop=(k == TPB - 1))
                last.then_inc(A["s"], 1)
                for c in range(CH):
                    for k in range(TPB):
                        last = T.transpose(pB[:, (c * TPB + k) * P:(c * TPB + k + 1) * P],
                                           a_sw[:, k, c * P:(c + 1) * P], ident[:, :])
                last.then_inc(A["swTp"], 1)

            def att_snT(b):
                pe.wait_ge(A["sn"], b + 1)
                for c in range(CH):
                    T.transpose(pA[:, c * P:(c + 1) * P], a_sn[:, c, 0:D], ident[:, :])
                    last = T.matmul(pA[0:1, 256 + c * P:256 + (c + 1) * P], a_sn[:, c, D:D + 1], ident[:, :],
                                    start=True, stop=True)
                last.then_inc(A["snTp"], 1)

            def att_st(b):
                pe.wait_ge(setup_v, 6)
                pe.wait_ge(A["snT"], b + 1)
                for h in range(H):
                    o = pC[0:DH, h * M:(h + 1) * M]
                    T.matmul(o, wfxT_sb[:, h * DH:(h + 1) * DH], a_snT[:, h * M:(h + 1) * M], start=True, stop=False)
                    last = T.matmul(o, bfx_sb[0:1, h * DH:(h + 1) * DH], a_nnT[0:1, h * M:(h + 1) * M],
                                    start=False, stop=True)
                last.then_inc(A["stp"], 1)

            def att_uv(b):
                pe.wait_ge(setup_v, 6)
                pe.wait_ge(A["stT"], b + 1)
                T.matmul(pC[0:DH, 256:512], mqk[:, :], a_stT[:, :], start=True, stop=True)
                for h in range(H):
                    c, j = divmod(h, HPC)
                    last = T.matmul(pA[32 * j:32 * j + 32, c * D:(c + 1) * D], a_stT[:, h * M:(h + 1) * M],
                                    vw[:, h, :], start=True, stop=True)
                last.then_inc(A["up"], 1)

            def att_scores(b):
                pe.wait_ge(setup_v, 6)
                pe.wait_ge(A["uT"], b + 1)
                for h in range(H):
                    c, j = divmod(h, HPC)
                    last = T.matmul(pA[32 * j:32 * j + 32, 256 + c * M:256 + (c + 1) * M],
                                    a_uT[:, h * M:(h + 1) * M], a_stT[:, h * M:(h + 1) * M], start=True, stop=True)
                last.then_inc(A["scp"], 1)

            def att_mix(b):
                pe.wait_ge(setup_v, 6)
                pe.wait_ge(A["atT"], b + 1)
                for h in range(H):
                    c, j = divmod(h, HPC)
                    last = T.matmul(pC[32 * j:32 * j + 32, c * D:(c + 1) * D], a_atT[32 * j:32 * j + 32, c, :],
                                    a_sv[32 * j:32 * j + 32, c, :], start=True, stop=True)
                last.then_inc(A["pp"], 1)

            def att_out(b):
                pe.wait_ge(A["p"], b + 1)
                for k in range(TPB):
                    o = pB[:, k * D:(k + 1) * D]
                    for c in range(CH):
                        T.matmul(o, a_swT[:, c, k * P:(k + 1) * P], a_p[:, c, :], start=(c == 0), stop=False)
                    last = row_bias(o, BOUT, D)
                last.then_inc(A["op"], 1)

            def mix_transpose(tm):
                pe.wait_ge(S["res"], tm)
                pe.wait_ge(S["act"], tm + 1)
                T.transpose(pA[:, 384:512], act[:, :], ident[:, :]).then_inc(S["actTp"], 1)

            def scatter(ts):
                pe.wait_ge(S["ohw"], ts + 1)
                pe.wait_ge(S["ohl"], ts + 1)
                for c in range(NG):
                    for j in range(4):
                        first = c * 4 + j
                        last = T.matmul(pT[32 * j:32 * j + 32, c * GRP * LO:(c + 1) * GRP * LO],
                                        ohw[:, first, :, :].rearrange("p h g -> p (h g)"),
                                        ohl[:, :, first:P:P // GRP].rearrange("p l t -> p t l"), start=True, stop=True)
                last.then_inc(S["sctp"], 1)

            def mix(tm):
                pe.wait_ge(S["actT"], tm + 1)
                T.matmul(pA[:, 384:512], actT[:, :], up_sb[:, :], start=True, stop=True).then_inc(S["mix"], 1)

            def slot(i, k, on):
                att, q_on, late_on, _, _, sc_on, mix_on, _ = on
                b = i + 1
                t0, t1, _, _, ts, tm = (2 * i + k - n for n in range(6))
                if q_on:
                    if k == 0:
                        pe.wait_ge(F["gate"], i)
                    pe.wait_ge(F["x2"], t0 + 1)
                    T.transpose(pM[:, 0:P], x2[k][:, :], ident[:, :]).then_inc(F["x2Tp"], 1)
                if sc_on:
                    pe.wait_ge(S["wn"], ts + 1)
                    pe.wait_ge(S["hl"], ts + 1)
                    pe.wait_ge(S["sct"], ts)
                    T.transpose(pT[:, 0:P], wn[:, :, :].rearrange("p h n -> p (h n)"), ident[:, :])
                    for n in range(2):
                        last = T.transpose(pT[:, (n + 1) * P:(n + 2) * P], hl[k][:, n, :], ident[:, :])
                    last.then_inc(S["t3p"], 1)
                if att and k == 1 and mix_on:
                    pe.wait_ge(S["res"], tm)
                if q_on:
                    pe.wait_ge(F["x2T"], t0 + 1)
                    for c in range(4):
                        last = T.matmul(pQ[:, c * P:(c + 1) * P], wqc[:, 2 * c:2 * c + 2, :].rearrange("p h d -> p (h d)"),
                                        x2T[k][:, :], start=True, stop=True)
                    last.then_inc(F["qc"], 1)
                if q_on:
                    if late_on:
                        pe.wait_ge(F["y"], t1)
                    T.matmul(pS[:, 0:INNER], x2T[k][:, :], wqg[:, :, :], start=True, stop=False)
                    row_bias(pS[:, 0:INNER], BQG, INNER).then_inc(F["q"], 1)
                    T.matmul(pM[:, P + k * P:2 * P + k * P], x2T[k][:, :], downT_sb[:, :],
                             start=True, stop=True).then_inc(F["inner"], 1)
                    pe.wait_ge(F["sq"], t0 + 1)
                    pe.wait_ge(F["ss"], t0)
                    if sc_on:
                        pe.wait_ge(S["t3"], ts + 1)
                    for c in range(4):
                        last = T.matmul(pT[:, 384 + 2 * c:386 + 2 * c], q_sq[:, c, :], half_c[:, :], start=True, stop=True)
                    last.then_inc(F["ssp"], 1)
                if att and k == 1:
                    att_st(b)
                if att and k == 0:
                    if mix_on:
                        pe.wait_ge(S["res"], tm)
                    att_xT(b)
                if att and k == 1:
                    att_uv(b)
                if late_on:
                    pe.wait_ge(F["qn"], t1 + 1)
                    if q_on:
                        pe.wait_ge(F["sq"], t0 + 1)
                    for c in range(4):
                        last = T.transpose(pQ[:, c * P:(c + 1) * P],
                                           q_n[:, 4 * c:4 * c + 4, :].rearrange("p l d -> p (l d)"), ident[:, :])
                    last.then_inc(F["qnTp"], 1)
                if att and k == 0:
                    att_logits(b)
                if att and k == 1:
                    att_scores(b)
                if sc_on and k == 0:
                    scatter(ts)
                if late_on:
                    pe.wait_ge(F["qnT"], t1 + 1)
                    if q_on:
                        pe.wait_ge(F["qr"], t0 + 1)
                    for c in range(4):
                        for n in range(2):
                            at = (n * 4 + c) * 2 * PK
                            last = T.matmul(pS[:, at:at + 2 * PK], q_nT[64 * n:64 * n + 64, c, :],
                                            kb[64 * n:64 * n + 64, :, :], start=True, stop=True)
                    last.then_inc(F["sc"], 1)
                if att and k == 1:
                    att_mix(b)
                if mix_on and k == 1:
                    mix_transpose(tm)
                if mix_on and k == 0:
                    mix_transpose(tm)
                if att and k == 1:
                    att_out(b)
                if mix_on:
                    mix(tm)
                if sc_on and k == 1:
                    scatter(ts)
                if att and k == 0:
                    att_slice(b)
                if att and k == 0:
                    if mix_on:
                        pe.wait_ge(S["res"], tm + 1)
                    att_snT(b)

            for i in range(FIRST, LOOP0):
                for k in range(2):
                    slot(i, k, stages(i, k))
            with pe.Fori(LOOP0, LOOP1) as i:
                for k in range(2):
                    slot(i, k, stages(None, k))
            for i in range(LOOP1, LAST + 1):
                for k in range(2):
                    slot(i, k, stages(i, k))

        @block.scalar
        def _(ac):
            C = nc.scalar

            def copy(o, i_):
                return C.activation(o, i_, ACT.Copy)

            def att_xT(b):
                ac.wait_ge(A["xTp"], b + 1)
                copy(a_xT[:, :, :].rearrange("p t n -> p (t n)"), pA[:, 0:TPB * P]).then_inc(A["xT"], 1)

            def att_exp(b):
                ac.wait_ge(A["sub"], b + 1)
                C.activation(a_e[:, :, :], a_e[:, :, :], ACT.Exp).then_inc(A["exp"], 1)

            def att_swT(b):
                ac.wait_ge(A["swTp"], b + 1)
                copy(a_swT[:, :, :].rearrange("p c n -> p (c n)"), pB[:, :]).then_inc(A["swT"], 1)

            def att_snT(b):
                ac.wait_ge(A["snTp"], b + 1)
                copy(a_snT[:, :], pA[:, 0:HM])
                copy(a_nnT[:, :], pA[0:1, 256:256 + HM]).then_inc(A["snT"], 1)

            def att_stT(b):
                ac.wait_ge(A["stp"], b + 1)
                copy(a_stT[:, :], pC[0:DH, 0:HM]).then_inc(A["stT"], 1)

            def att_uT(b):
                ac.wait_ge(A["up"], b + 1)
                copy(a_uT[:, :], pC[0:DH, 256:512])
                copy(a_sv[:, :, :].rearrange("p c d -> p (c d)"), pA[:, 0:CH * D]).then_inc(A["uT"], 1)

            def att_sexp(b):
                ac.wait_ge(A["ssub"], b + 1)
                C.activation(a_se[:, :, :], a_se[:, :, :], ACT.Exp, scale=DH ** -0.5).then_inc(A["sexp"], 1)

            def att_p(b):
                ac.wait_ge(A["pp"], b + 1)
                copy(a_p[:, :, :].rearrange("p c d -> p (c d)"), pC[:, 0:CH * D]).then_inc(A["p"], 1)

            def scattered(ts):
                ac.wait_ge(S["sctp"], ts + 1)
                ac.wait_ge(spilled, 16 * GRP * ts)
                copy(sct[:, :, :].rearrange("p c n -> p (c n)"), pT[:, :]).then_inc(S["sct"], 1)

            def low_rows(ts):
                ac.wait_ge(S["ohlb"], ts + 1)
                ac.wait_ge(S["sctp"], ts)
                copy(ohl[:, :, :].rearrange("p l t -> p (l t)"),
                     ohlb[:, :, :].rearrange("p l t -> p (l t)")).then_inc(S["ohl"], 1)

            def slot(i, k, on):
                att, q_on, late_on, _, pair_on, sc_on, mix_on, _ = on
                b, kk = i + 1, 1 - k
                t0, t1, _, tp, ts, tm = (2 * i + k - n for n in range(6))
                if q_on:
                    ac.wait_ge(F["x2Tp"], t0 + 1)
                    copy(x2T[k][:, :], pM[:, 0:P]).then_inc(F["x2T"], 1)
                if sc_on:
                    ac.wait_ge(S["t3p"], ts + 1)
                    ac.wait_ge(S["ohlb"], ts)
                    copy(t3[:, :, :].rearrange("p n t -> p (n t)"), pT[:, 0:2 * P])
                    copy(lo_t[:, :], pT[:, 2 * P:3 * P]).then_inc(S["t3"], 1)
                if q_on:
                    ac.wait_ge(F["qc"], t0 + 1)
                    for c in range(4):
                        last = C.activation(q_sq[:, c, :], pQ[:, c * P:(c + 1) * P], ACT.Square, bias=bqcT[:, c:c + 1])
                    last.then_inc(F["sq"], 1)
                if q_on and k == 1:
                    ac.wait_ge(F["inner"], t0 + 1)
                    C.activation(gate[:, ds(t0 - 1, 2), :].rearrange("p t e -> p (t e)"), pM[:, P:3 * P],
                                 ACT.Gelu).then_inc(F["gate"], 1)
                    C.activation(warm[:, :], exp_bias[:, :], ACT.Exp)
                if att and k == 1:
                    att_stT(b)
                if att and k == 0:
                    att_xT(b)
                if att and k == 1:
                    att_uT(b)
                if late_on:
                    ac.wait_ge(F["qnTp"], t1 + 1)
                    copy(q_nT[:, :, :].rearrange("p c t -> p (c t)"), pQ[:, :]).then_inc(F["qnT"], 1)
                if att and k == 1:
                    att_sexp(b)
                if sc_on and k == 0:
                    low_rows(ts)
                if att and k == 0:
                    att_exp(b)
                if sc_on and k == 0:
                    scattered(ts)
                if q_on:
                    ac.wait_ge(F["q1"], t0 + 1)
                    C.activation(q_sq2[:, :, :].rearrange("p l d -> p (l d)"),
                                 q_1[:, :, :].rearrange("p h d -> p (h d)"), ACT.Square).then_inc(F["sq2"], 1)
                if sc_on and k == 1:
                    low_rows(ts)
                if late_on:
                    ac.wait_ge(F["sc"], t1 + 1)
                    for n in range(2):
                        last = C.activation(y[kk][:, n * 512:(n + 1) * 512], pS[:, n * 512:(n + 1) * 512],
                                            ACT.Identity, bias=one_bias[:, :], scale=UNIT)
                    last.then_inc(F["y"], 1)
                if att and k == 1:
                    att_p(b)
                if mix_on:
                    ac.wait_ge(S["actTp"], tm + 1)
                    copy(actT[:, :], pA[:, 384:512]).then_inc(S["actT"], 1)
                if pair_on:
                    ac.wait_ge(S["dec"], tp + 1)
                    C.activation(wexp[kk][:, :, :].rearrange("p h n -> p (h n)"), valb[:, :], ACT.Exp,
                                 bias=exp_bias[:, :], scale=1.0 / UNIT).then_inc(S["wexp"], 1)
                    copy(hl[kk][:, :, :].rearrange("p n j -> p (n j)"),
                         hlb[:, :, :].rearrange("p n j -> p (n j)")).then_inc(S["hl"], 1)
                if sc_on and k == 1:
                    scattered(ts)
                if att and k == 0:
                    att_swT(b)
                if att and k == 0:
                    att_snT(b)

            ac.wait_ge(setup_a, 2)
            copy(bqcT[:, :], pM[:, 0:4]).then_inc(setup_b, 1)

            for i in range(FIRST, LOOP0):
                for k in range(2):
                    slot(i, k, stages(i, k))
            with ac.Fori(LOOP0, LOOP1) as i:
                for k in range(2):
                    slot(i, k, stages(None, k))
            for i in range(LOOP1, LAST + 1):
                for k in range(2):
                    slot(i, k, stages(i, k))


def kernel(**inputs):
    import numpy as np
    import concourse.bacc as bacc
    from concourse import mybir as mb
    from concourse.bass_utils import run_bass_kernel_spmd

    a = {n: np.asarray(v) for n, v in inputs.items()}
    x = a["x"].astype(np.int32)
    B, N = x.shape
    D = a["L0_tok_weight"].shape[1]
    P, DH, PK = 128, a["L0_attn_Wslice"].shape[1], a["L0_ffn_keys0"].shape[0]
    arrays = [
        ("ids", x.reshape(-1, P).T), ("tok", a["L0_tok_weight"]), ("wx", a["L0_attn_Wx"]), ("wfxT", a["L0_attn_Wfx"].T),
        ("wsT", a["L0_attn_Wslice"].T), ("bxT", a["L0_attn_bx"].reshape(-1, DH).T), ("bfx", a["L0_attn_bfx"][None]),
        ("bslice", a["L0_attn_bslice"][None]), ("attn_wq", a["L0_attn_Wq"]), ("attn_wk", a["L0_attn_Wk"]),
        ("attn_wv", a["L0_attn_Wv"]), ("woutT", a["L0_attn_Wout"].T), ("bout", a["L0_attn_bout"][None]),
        ("temperature", a["L0_attn_temperature"].reshape(1, -1)), ("ffn_wqT", a["L0_ffn_Wq"].T),
        ("bq", a["L0_ffn_bq"][None]), ("ln_g", a["L0_ffn_ln_g"][None]), ("ln_b", a["L0_ffn_ln_b"][None]),
        ("keys0", a["L0_ffn_keys0"]), ("keys1", a["L0_ffn_keys1"]), ("downT", a["L0_ffn_expert_down"][:2 * PK].T),
        ("up", a["L0_ffn_expert_up"]),
    ]
    nc = bacc.Bacc("TRN2", target_bir_lowering=False, num_devices=1)
    feed, args = {}, []
    for name, v in arrays:
        v = np.ascontiguousarray(v)
        feed[name + "_dram"] = v
        args.append(nc.dram_tensor(name + "_dram", v.shape, mb.dt.from_np(v.dtype), kind="ExternalInput").ap())
    args.append(nc.dram_tensor("out_dram", (B * N, D), mb.dt.float32, kind="ExternalOutput").ap())
    tower_program(nc, *args)
    r = run_bass_kernel_spmd(nc, [feed], core_ids=[0])
    return r.results[0]["out_dram"].reshape(B, N, D)
```

```python
import concourse.bass as bass
import concourse.mybir as mybir
from contextlib import ExitStack


def tower_program(nc, ids, tok, wx, wfxT, wsT, bxT, bfx, bslice, attn_wq, attn_wk, attn_wv, woutT, bout,
                  temperature, ffn_wqT, bq, ln_g, ln_b, keys0, keys1, downT, up, out):
    F32, I32, BF16 = mybir.dt.float32, mybir.dt.int32, mybir.dt.bfloat16
    ALU, ACT, AX = mybir.AluOpType, mybir.ActivationFunctionType, mybir.AxisListType.X
    ds = bass.ds

    P = 128
    TILES = ids.shape[1]
    D = tok.shape[1]
    TPB = 2
    BATCHES = TILES // TPB
    H = temperature.shape[1]
    DH = wsT.shape[0]
    M = wsT.shape[1]
    HM = H * M
    CH = HM // P
    HPC = H // CH
    INNER = H * DH
    PK = keys0.shape[0]
    HALF = keys0.shape[1]
    K = 16
    HS = 2 * H
    E = 2 * PK
    LO = 16
    HI = E // LO
    EPS = 1e-5

    IDX = 7
    UNIT = float(2 ** 23) * 1000 / 1024
    ONE = float(2 ** 23)
    TOP = 2 ** 31 - 2 ** 24
    LEAST = 2.0 ** -126
    RECTS = [(0, 1, 0, 16), (1, 16, 0, 1), (1, 2, 1, 8), (2, 8, 1, 2), (2, 5, 2, 5)]
    NC = sum((a1 - a0) * (b1 - b0) for a0, a1, b0, b1 in RECTS)

    GRP = 4
    NG = P // GRP // 4

    BQG, BLG, BOUT = 0, INNER, INNER + HM
    ROWS = BOUT + D

    ctx = ExitStack()
    with ctx:
        def sb(name, shape, dt=F32):
            return ctx.enter_context(nc.sbuf_tensor(name, shape, dt))

        def ps(name, shape=(P, 512)):
            return ctx.enter_context(nc.psum_tensor(name, list(shape), F32))

        def sem(name):
            return ctx.enter_context(nc.semaphore(name))

        ident = sb("ident", [P, P])
        ones = sb("ones", [1, 1])
        pick = sb("pick", [96, P], BF16)
        rows = sb("rows", [1, ROWS])
        bqc_row = sb("bqc_row", [1, INNER])
        bqcT = sb("bqcT", [P, 4])
        half_c = sb("half_c", [P, 2])
        rest = sb("rest", [1, 2, ROWS])
        parts = sb("parts", [96, ROWS], BF16)
        idx_iota = sb("idx_iota", [P, PK], I32)
        lo_iota = sb("lo_iota", [P, LO, P], BF16)
        eps_c = sb("eps_c", [P, HS])
        mhalf_c = sb("mhalf_c", [P, HS])
        top_c = sb("top_c", [P, H], I32)
        one_bias = sb("one_bias", [P, 1])
        exp_bias = sb("exp_bias", [P, 1])
        warm = sb("warm", [P, 1])
        spare = sb("spare", [P, 2])
        ids_sb = sb("ids_sb", [P, TILES], I32)
        wx_sb = sb("wx_sb", [DH, H, D])
        wfxT_sb = sb("wfxT_sb", [D, INNER])
        wsT_sb = sb("wsT_sb", [DH, M])
        bxT_sb = sb("bxT_sb", [DH, H])
        bfx_sb = sb("bfx_sb", [1, INNER])
        bsl_sb = sb("bsl_sb", [1, M])
        aq_sb = sb("aq_sb", [DH, DH])
        ak_sb = sb("ak_sb", [DH, DH])
        av_sb = sb("av_sb", [DH, DH])
        wout_sb = sb("wout_sb", [DH, H, D])
        temp_sb = sb("temp_sb", [P, H])
        rtemp = sb("rtemp", [P, H])
        lw = sb("lw", [D, HM])
        mqk = sb("mqk", [DH, DH])
        vw = sb("vw", [DH, H, D])
        wqT_sb = sb("wqT_sb", [D, H, DH])
        bq_sb = sb("bq_sb", [1, H, DH])
        g_sb = sb("g_sb", [P, DH])
        b_sb = sb("b_sb", [P, DH])
        wmean = sb("wmean", [P, 2, H])
        wqc = sb("wqc", [D, H, DH])
        wqg = sb("wqg", [D, H, DH])
        k_raw = sb("k_raw", [PK, 2, HALF])
        k_sq = sb("k_sq", [PK, 2, HALF])
        k_ss = sb("k_ss", [PK, 2])
        k_rn = sb("k_rn", [PK, 2])
        k_unit = sb("k_unit", [PK, 2, 2, HALF])
        kb = sb("kb", [P, 2, PK])
        downT_sb = sb("downT_sb", [D, E])
        up_sb = sb("up_sb", [E, D])

        h_all = sb("h_all", [P, TILES, D])
        gate = sb("gate", [P, TILES, E])

        a_st = sb("a_st", [P, TILES, 6])
        a_mv = sb("a_mv", [P, TILES, 2])
        a_rs = sb("a_rs", [P, TILES])
        a_x = sb("a_x", [P, TPB, D + 1])
        a_xT = sb("a_xT", [P, TPB, P])
        a_mx = sb("a_mx", [P, TPB * H])
        a_e = sb("a_e", [P, TPB * H, M])
        a_sum = sb("a_sum", [P, TPB * H])
        a_rsum = sb("a_rsum", [P, TPB * H])
        a_sw = sb("a_sw", [P, TPB, HM])
        a_swT = sb("a_swT", [P, CH, TPB * P])
        a_den = sb("a_den", [P, CH])
        a_rden = sb("a_rden", [P, CH])
        a_sn = sb("a_sn", [P, CH, D + 1])
        a_snT = sb("a_snT", [P, HM])
        a_nnT = sb("a_nnT", [1, HM])
        a_stT = sb("a_stT", [DH, HM])
        a_uT = sb("a_uT", [DH, HM])
        a_sv = sb("a_sv", [P, CH, D])
        a_smx = sb("a_smx", [P, CH])
        a_se = sb("a_se", [P, CH, M])
        a_ssum = sb("a_ssum", [P, CH])
        a_srs = sb("a_srs", [P, CH])
        a_at = sb("a_at", [P, CH, M])
        a_atT = sb("a_atT", [P, CH, M])
        a_p = sb("a_p", [P, CH, D])

        l_st = sb("l_st", [P, TPB, 6])
        l_mv = sb("l_mv", [P, TPB, 2])
        l_rs = sb("l_rs", [P, TPB])
        x2 = [sb(f"x2_{k}", [P, D]) for k in range(2)]
        x2T = [sb(f"x2T_{k}", [P, P]) for k in range(2)]
        q_sq = sb("q_sq", [P, 4, P])
        q_ss = sb("q_ss", [P, H])
        q_rs = sb("q_rs", [P, H])
        q_r = sb("q_r", [P, H, DH])
        q_1 = sb("q_1", [P, H, DH])
        q_sq2 = sb("q_sq2", [P, HS, HALF])
        q_ss2 = sb("q_ss2", [P, HS])
        q_t2 = sb("q_t2", [P, HS])
        q_rn = sb("q_rn", [P, HS])
        q_n = sb("q_n", [P, HS, HALF])
        q_nT = sb("q_nT", [P, 4, P])
        y = [sb(f"y{k}", [P, HS * PK], I32) for k in range(2)]

        key = sb("key", [P, HS, PK])
        keylt = sb("keylt", [P, HS, PK])
        keym = sb("keym", [P, HS, PK])
        best = [sb(f"best{k}", [P, HS, K]) for k in range(2)]
        base = [sb(f"base{k}", [P, HS], I32) for k in range(2)]
        based = sb("based", [P, H], I32)
        rel = sb("rel", [P, HS, K], I32)
        cand = sb("cand", [P, H, NC], I32)
        candc = sb("candc", [P, H, NC])
        candlt = sb("candlt", [P, H, NC])
        candm = sb("candm", [P, H, NC])
        win = sb("win", [P, H, K])
        valb = sb("valb", [P, H * K], I32)
        hlb = sb("hlb", [P, 2, H * K], I32)
        wexp = [sb(f"wexp{k}", [P, H, K]) for k in range(2)]
        hl = [sb(f"hl{k}", [P, 2, H * K]) for k in range(2)]
        wsum = sb("wsum", [P, H])
        wrec = sb("wrec", [P, H])
        wn = sb("wn", [P, H, K])
        t3 = sb("t3", [P, 2, P])
        lo_t = sb("lo_t", [P, P], BF16)
        ohlb = sb("ohlb", [P, LO, P], BF16)
        ohl = sb("ohl", [P, LO, P])
        ohw = sb("ohw", [P, P // GRP, HI, GRP])
        sct = sb("sct", [P, NG, GRP * LO])
        wacc = [sb(f"wacc{k}", [P, E]) for k in range(2)]
        act = sb("act", [P, E])
        actT = sb("actT", [P, P])
        res = [sb(f"res{k}", [P, D]) for k in range(2)]

        pA, pB, pC = ps("pA"), ps("pB"), ps("pC")
        pM = ps("pM")
        pQ = ps("pQ")
        pS = ps("pS", [P, 1024])
        pT = ps("pT")

        logit_loads = sem("logit_loads"); query_loads = sem("query_loads"); other_loads = sem("other_loads")
        ids_in = sem("ids_in"); gathered0 = sem("gathered0"); gathered = sem("gathered")
        pc = sem("pc"); setup_v = sem("setup_v"); setup_p = sem("setup_p"); setup_t = sem("setup_t")
        setup_a = sem("setup_a"); setup_b = sem("setup_b"); setup_o = sem("setup_o")
        A = {n: sem("a_" + n + "_done") for n in (
            "st", "mv", "t", "rs", "x", "xTp", "xT", "lg", "mx", "sub", "exp", "sum", "rsum", "sw", "s", "swTp", "swT",
            "den", "rden", "sn", "snTp", "snT", "stp", "stT", "up", "uT", "scp", "smx", "ssub", "sexp", "ssum",
            "srs", "at", "atT", "pp", "p", "op", "h2")}
        F = {n: sem("f_" + n + "_done") for n in (
            "st", "mv", "t", "rs", "x2", "x2Tp", "x2T", "qc", "q", "inner", "ssp", "sq", "gate", "ss", "t2", "rq", "qr", "q1",
            "sq2", "ss2", "t3", "rn", "qn", "qnTp", "qnT", "sc", "y")}
        S = {n: sem("s_" + n + "_done") for n in (
            "key", "first", "lt", "mask", "second", "base", "based", "rel", "cand", "clamp", "wfirst", "wlt", "wmask", "wsecond",
            "dec", "wexp", "hl", "wsum", "wrec", "wn", "t3p", "t3", "ohlb", "ohl", "ohw", "sctp", "sct",
            "act", "actTp", "actT", "mix", "res")}
        spilled = sem("spilled")
        wacc_in = [sem(f"wacc_in{k}") for k in range(2)]
        stored = [sem(f"stored{k}") for k in range(2)]

        LOGIT_LOADS = [
            (wx_sb[:, :, :], wx.rearrange("(h d) i -> d h i", d=DH)), (wsT_sb[:, :], wsT), (bxT_sb[:, :], bxT),
            (bsl_sb[:, :], bslice), (temp_sb[:, :], temperature.partition_broadcast(P)), (rows[:, BOUT:ROWS], bout)]
        QUERY_LOADS = [
            (wqT_sb[:, :, :], ffn_wqT.rearrange("p (h d) -> p h d", d=DH)),
            (bq_sb[:, :, :], bq.rearrange("p (h d) -> p h d", d=DH)), (g_sb[:, :], ln_g.partition_broadcast(P)),
            (k_raw[:, 0, :], keys0), (k_raw[:, 1, :], keys1), (b_sb[:, :], ln_b.partition_broadcast(P)),
            (aq_sb[:, :], attn_wq), (ak_sb[:, :], attn_wk), (av_sb[:, :], attn_wv)]
        OTHER_LOADS = [
            (wout_sb[:, :, :], woutT.rearrange("(h i) o -> i h o", i=DH)), (wfxT_sb[:, :], wfxT), (bfx_sb[:, :], bfx),
            (downT_sb[:, :], downT), (up_sb[:, :], up[0:E, :])]

        FIRST, LAST = -1, BATCHES + 2
        EAGER = 1
        LONE = 2
        LOOP0, LOOP1 = 3, BATCHES - 1

        def by_group(row):
            return row.rearrange("p (g n) -> p n g", g=GRP)

        def triples(on):
            return pT if on[2] else pQ

        def held(on):
            return on[6] and on[5] and on[4] and not on[1]

        def held_before(i, k):
            return isinstance(i, int) and i >= LOOP1 and held(stages(i - 1 + k, 1 - k))

        def stages(i, k):
            if i is None:
                return (True,) * 8
            t = [2 * i + k - n for n in range(6)]
            return (i + 1 < BATCHES, *[0 <= x < TILES for x in t], 0 <= t[0] + 1 < TILES)

        scratch = [nc.dram_tensor(f"scratch{k}", [P, E], F32, kind="Internal").ap() for k in range(2)]
        block = ctx.enter_context(nc.Block())

        @block.sync
        def _(sp):
            sp.dma_start(ids_sb[:, :], ids).then_inc(ids_in, 16)
            for dst, src in LOGIT_LOADS:
                sp.dma_start(dst, src).then_inc(logit_loads, 16)
            for dst, src in OTHER_LOADS:
                sp.dma_start(dst, src).then_inc(other_loads, 16)

            def slot(i, k, on):
                sc_on, mix_on = on[5:7]
                t4, t5 = 2 * i + k - 4, 2 * i + k - 5
                if sc_on:
                    sp.wait_ge(S["sct"], t4 + 1)
                    for g in range(GRP):
                        sp.dma_start(
                            scratch[k].rearrange("(g c j) (h l) -> g (j h) c l", g=GRP, c=NG, l=LO)[g],
                            sct[g:P:GRP, :, g * LO:(g + 1) * LO]).then_inc(spilled, 16)
                if mix_on and on[1]:
                    sp.wait_ge(S["res"], t5 + 1)
                    sp.dma_start(out[ds(t5 * P, P), :], res[1 - k][:, :]).then_inc(stored[1 - k], 16)
                if sc_on:
                    sp.wait_ge(spilled, 16 * GRP * (t4 + 1))
                    if mix_on:
                        sp.wait_ge(S["act"], t5)
                    sp.dma_start(wacc[k][:, :], scratch[k]).then_inc(wacc_in[k], 16)
                if mix_on and not on[1]:
                    sp.wait_ge(S["res"], t5 + 1)
                    sp.dma_start(out[ds(t5 * P, P), :], res[1 - k][:, :]).then_inc(stored[1 - k], 16)

            for i in range(FIRST, LOOP0):
                for k in range(2):
                    slot(i, k, stages(i, k))
            with sp.Fori(LOOP0, LOOP1) as i:
                for k in range(2):
                    slot(i, k, stages(None, k))
            for i in range(LOOP1, LAST + 1):
                for k in range(2):
                    slot(i, k, stages(i, k))
            for k in range(2):
                sp.wait_ge(stored[k], 16 * (TILES // 2))

        @block.gpsimd
        def _(gp):
            G = nc.gpsimd
            G.memset(ident[:, :], 0.0).then_inc(pc, 1)
            gp.wait_ge(pc, 1)
            G.affine_select(out=ident[:, :], in_=ident[:, :], compare_op=ALU.not_equal, fill=1.0, base=0,
                            pattern=[[-1, P]], channel_multiplier=1).then_inc(pc, 1)
            gp.wait_ge(ids_in, 16)

            def gather(t, arrived):
                G.indirect_dma_start(h_all[:, t, :], None, tok[:, :],
                                     bass.IndirectOffsetOnAxis(ap=ids_sb[:, t:t + 1], axis=0)).then_inc(arrived, 16)

            for t in range(TPB):
                gather(t, gathered0)
            for t in range(TPB, 2 * TPB):
                gather(t, gathered)
            G.memset(top_c[:, :], TOP)
            G.memset(eps_c[:, :], EPS)
            G.memset(mhalf_c[:, :], -0.5).then_inc(pc, 1)
            gp.wait_ge(pc, 3)

            def candidates(k, tl):
                bs = base[k][:, :].rearrange("p (h s) -> p h s", s=2)
                bt = best[k][:, :, :].bitcast(I32).rearrange("p (h s) n -> p h s n", s=2)
                rl = rel[:, :, :].rearrange("p (h s) n -> p h s n", s=2)
                gp.wait_ge(S["base"], tl + 1)
                G.tensor_tensor(based[:, :], bs[:, :, 1], top_c[:, :], ALU.subtract).then_inc(S["based"], 1)
                G.tensor_tensor(rl[:, :, 0, :], bt[:, :, 0, :],
                                bs[:, :, 0:1].broadcast_to([P, H, K]), ALU.subtract)
                gp.wait_ge(S["based"], tl + 1)
                G.tensor_tensor(rl[:, :, 1, :], bt[:, :, 1, :],
                                based[:, :].unsqueeze(2).broadcast_to([P, H, K]), ALU.subtract
                                ).then_inc(S["rel"], 1)
                gp.wait_ge(S["rel"], tl + 1)
                gp.wait_ge(S["clamp"], tl)
                at = 0
                for n, (a0, a1, b0, b1) in enumerate(RECTS):
                    na, nb = a1 - a0, b1 - b0
                    o = cand[:, :, at:at + na * nb].rearrange("p h (a b) -> p h a b", b=nb)
                    ins = G.tensor_tensor(
                        o, rl[:, :, 0, a0:a1].unsqueeze(3).broadcast_to([P, H, na, nb]),
                        rl[:, :, 1, b0:b1].unsqueeze(2).broadcast_to([P, H, na, nb]), ALU.add)
                    at += na * nb
                ins.then_inc(S["cand"], 1)

            def att_deviation(n, tiles):
                gp.wait_ge(A["mv"], n)
                G.tensor_tensor(a_rs[:, tiles], a_mv[:, tiles, 1], eps_c[:, tiles], ALU.add).then_inc(A["t"], 1)
                gp.wait_ge(A["t"], n)
                G.tensor_tensor(a_rs[:, tiles], a_rs[:, tiles], mhalf_c[:, tiles], ALU.pow).then_inc(A["rs"], 1)

            def deviation(t0):
                gp.wait_ge(F["ss"], t0 + 1)
                G.tensor_tensor(q_rs[:, :], q_ss[:, :], mhalf_c[:, 0:H], ALU.pow).then_inc(F["rq"], 1)

            def unit_halves(t0):
                gp.wait_ge(F["ss2"], t0 + 1)
                G.tensor_tensor(q_rn[:, :], q_ss2[:, :], mhalf_c[:, :], ALU.pow).then_inc(F["rn"], 1)
                gp.wait_ge(F["rn"], t0 + 1)
                G.tensor_tensor(q_n[:, :, :], q_1[:, :, :].rearrange("p h (s d) -> p (h s) d", d=HALF),
                                q_rn[:, :].unsqueeze(2).broadcast_to([P, HS, HALF]),
                                ALU.mult).then_inc(F["qn"], 1)

            def slot(i, k, on):
                att, q_on, _, list_on, pair_on, sc_on, mix_on, _ = on
                b, kk = i + 1, 1 - k
                t0, _, tl, tp, ts, tm = (2 * i + k - n for n in range(6))
                if list_on:
                    gp.wait_ge(S["lt"], tl + 1)
                    gp.wait_ge(S["second"], tl)
                    G.tensor_tensor(keym[:, :, :], key[:, :, :], keylt[:, :, :], ALU.mult).then_inc(S["mask"], 1)
                if q_on:
                    deviation(t0)
                if q_on:
                    gp.wait_ge(F["qr"], t0 + 1)
                    G.tensor_tensor(q_1[:, :, :], q_r[:, :, :], b_sb[:, :].unsqueeze(1).broadcast_to([P, H, DH]),
                                    ALU.add).then_inc(F["q1"], 1)
                if mix_on:
                    gp.wait_ge(wacc_in[kk], 16 * (i - 2 + k))
                    gp.wait_ge(F["gate"], i - 2 + k)
                    gp.wait_ge(S["actTp"], tm)
                    G.tensor_tensor(act[:, :], wacc[kk][:, :], gate[:, ds(tm, 1), :], ALU.mult).then_inc(S["act"], 1)
                if list_on and k == 1:
                    candidates(k, tl)
                if q_on and k == 1:
                    unit_halves(t0)
                if att and k == 0:
                    gp.wait_ge(A["rsum"], b + 1)
                    G.tensor_tensor(a_sw[:, :, :].rearrange("p t (h m) -> p (t h) m", m=M), a_e[:, :, :],
                                    a_rsum[:, :].unsqueeze(2).broadcast_to([P, TPB * H, M]),
                                    ALU.mult).then_inc(A["sw"], 1)
                if att and k == 1:
                    gp.wait_ge(F["mv"], b + 1)
                    G.tensor_tensor(l_rs[:, :], l_mv[:, :, 1], eps_c[:, 0:TPB], ALU.add).then_inc(F["t"], 1)
                    gp.wait_ge(F["t"], b + 1)
                    G.tensor_tensor(l_rs[:, :], l_rs[:, :], mhalf_c[:, 0:TPB], ALU.pow).then_inc(F["rs"], 1)
                if list_on and k == 0:
                    candidates(k, tl)
                if pair_on:
                    gp.wait_ge(S["wrec"], tp + 1)
                    gp.wait_ge(S["wexp"], tp + 1)
                    gp.wait_ge(S["t3p"], tp)
                    G.tensor_tensor(wn[:, :, :], wexp[kk][:, :, :],
                                    wrec[:, :].unsqueeze(2).broadcast_to([P, H, K]), ALU.mult).then_inc(S["wn"], 1)
                if q_on and k == 0:
                    unit_halves(t0)
                if list_on:
                    gp.wait_ge(S["wlt"], tl + 1)
                    gp.wait_ge(S["wsecond"], tl)
                    G.tensor_tensor(candm[:, :, :], candc[:, :, :], candlt[:, :, :], ALU.mult).then_inc(S["wmask"], 1)

            att_deviation(1, slice(0, TPB))
            for t in range(2 * TPB, TILES // 2):
                gather(t, gathered)
            gp.wait_ge(setup_v, 1)
            G.tensor_tensor(k_rn[:, :], k_ss[:, :], mhalf_c[0:PK, 0:2], ALU.pow).then_inc(setup_p, 1)
            for t in range(TILES // 2, TILES):
                gather(t, gathered)
            for i in range(FIRST, LOOP0):
                for k in range(2):
                    slot(i, k, stages(i, k))
                    if i == FIRST and k == 0:
                        G.iota(idx_iota[:, :], [[1, PK]], 0, 0)
                        G.iota(lo_iota[:, :, :], [[1, LO], [0, P]], 0, 0,
                               allow_small_or_imprecise_dtypes=True).then_inc(pc, 1)
                        att_deviation(2, slice(TPB, TILES))
            with gp.Fori(LOOP0, LOOP1) as i:
                for k in range(2):
                    slot(i, k, stages(None, k))
            for i in range(LOOP1, LAST + 1):
                for k in range(2):
                    slot(i, k, stages(i, k))

        @block.vector
        def _(dv):
            V = nc.vector
            bqc = bqc_row[:, :].rearrange("p (h d) -> p h d", d=DH)
            bqg = rows[:, BQG:BQG + INNER].rearrange("p (h d) -> p h d", d=DH)
            brow = rows[:, BLG:BLG + HM].rearrange("p (h m) -> p h m", m=M)
            V.memset(ones[:, :], 1.0).then_inc(setup_o, 1)
            V.memset(pick[:, :], 0.0)
            V.memset(parts[:, :], 0.0)
            V.memset(kb[:, :, :], 0.0)
            for h in range(2):
                V.memset(half_c[h * DH:(h + 1) * DH, h:h + 1], 1.0 / DH)
                V.memset(half_c[h * DH:(h + 1) * DH, 1 - h:2 - h], 0.0)
            V.memset(one_bias[:, :], ONE)
            V.memset(exp_bias[:, :], -float(TOP >> IDX) / UNIT)
            for k in range(TPB):
                V.memset(a_x[:, k, D:D + 1], 1.0)
            def att_stats(n, tiles, arrived, count):
                dv.wait_ge(arrived, count)
                for t in tiles:
                    last = V.bn_stats(a_st[:, t, :], h_all[:, t, :])
                last.then_inc(A["st"], 1)
                dv.wait_ge(A["st"], n)
                for t in tiles:
                    last = V.bn_aggr(a_mv[:, t, :], a_st[:, t, :])
                last.then_inc(A["mv"], 1)

            def att_norm(b):
                dv.wait_ge(A["rs"], 1 if isinstance(b, int) and b == 0 else 2)
                for k in range(TPB):
                    t = b * TPB + k
                    last = V.tensor_scalar(a_x[:, k, 0:D], h_all[:, ds(t, 1), :].squeeze(1), a_mv[:, ds(t, 1), 0:1].squeeze(1),
                                           a_rs[:, ds(t, 1)], ALU.subtract, ALU.mult)
                last.then_inc(A["x"], 1)

            att_stats(1, range(TPB), gathered0, 16 * TPB)
            att_norm(0)
            dv.wait_ge(query_loads, 16 * len(QUERY_LOADS))
            V.tensor_tensor(k_sq[:, :, :], k_raw[:, :, :], k_raw[:, :, :], ALU.mult)
            V.tensor_reduce(wmean[:, 0, :], wqT_sb[:, :, :], AX, ALU.add)
            V.tensor_reduce(wmean[0:1, 1, :], bq_sb[:, :, :], AX, ALU.add).then_inc(setup_t, 1)
            dv.wait_ge(setup_t, 1)
            V.tensor_reduce(k_rn[:, :], k_sq[:, :, :], AX, ALU.add)
            V.tensor_scalar(wmean[:, 0, :], wmean[:, 0, :], 1.0 / DH, None, ALU.mult)
            V.tensor_scalar(wmean[0:1, 1, :], wmean[0:1, 1, :], 1.0 / DH, None, ALU.mult).then_inc(setup_t, 1)
            dv.wait_ge(setup_t, 2)
            V.tensor_scalar(k_ss[:, :], k_rn[:, :], 1e-24, None, ALU.max).then_inc(setup_v, 1)
            V.tensor_tensor(wqc[:, :, :], wqT_sb[:, :, :], wmean[:, 0, :].unsqueeze(2).broadcast_to([D, H, DH]),
                            ALU.subtract)
            V.tensor_tensor(bqc, bq_sb[:, :, :], wmean[0:1, 1, :].unsqueeze(2).broadcast_to([1, H, DH]),
                            ALU.subtract).then_inc(setup_t, 1)
            dv.wait_ge(logit_loads, 16 * len(LOGIT_LOADS))
            V.reciprocal(rtemp[:, :], temp_sb[:, :]).then_inc(setup_t, 1)
            dv.wait_ge(setup_t, 4)
            dv.wait_ge(setup_p, 1)
            for s in range(2):
                for r in range(2):
                    V.tensor_scalar(k_unit[:, r, s, :], k_raw[:, s, :], k_rn[:, s:s + 1], None,
                                    ALU.mult).then_inc(setup_v, 1)
            dv.wait_ge(setup_a, 1)
            V.tensor_tensor(lw[:, :].rearrange("p (h m) -> p h m", m=M),
                            pA[:, 0:HM].rearrange("p (h m) -> p h m", m=M),
                            rtemp[:, :].unsqueeze(2).broadcast_to([D, H, M]), ALU.mult)
            V.tensor_tensor(brow,
                            pB[0:1, 0:HM].rearrange("p (h m) -> p h m", m=M),
                            rtemp[0:1, :].unsqueeze(2).broadcast_to([1, H, M]), ALU.mult)
            for n in range(3):
                last = V.memset(pick[32 * n:32 * n + 1, :], 1.0)
            last.then_inc(setup_t, 1)

            def split(done, c0, c1):
                for n in range(3):
                    dv.wait_ge(setup_t, done)
                    left = rows[:, c0:c1] if n == 0 else rest[:, n - 1, c0:c1]
                    V.tensor_copy(parts[32 * n:32 * n + 1, c0:c1], left).then_inc(setup_t if n < 2 else setup_v, 1)
                    if n < 2:
                        dv.wait_ge(setup_t, done + 1)
                        V.tensor_tensor(rest[:, n, c0:c1], left, parts[32 * n:32 * n + 1, c0:c1],
                                        ALU.subtract).then_inc(setup_t, 1)
                        done += 2

            split(5, BLG, ROWS)

            lg = pB[:, :].rearrange("p (g m) -> p g m", m=M)

            def att_max(b):
                dv.wait_ge(A["lg"], b + 1)
                V.tensor_reduce(a_mx[:, :], lg, AX, ALU.max).then_inc(A["mx"], 1)

            def att_sub(b):
                dv.wait_ge(A["mx"], b + 1)
                V.tensor_tensor(a_e[:, :, :], lg, a_mx[:, :].unsqueeze(2).broadcast_to([P, TPB * H, M]),
                                ALU.subtract).then_inc(A["sub"], 1)

            def att_sum(b):
                dv.wait_ge(A["exp"], b + 1)
                V.tensor_reduce(a_sum[:, :], a_e[:, :, :], AX, ALU.add).then_inc(A["sum"], 1)

            def att_rsum(b):
                dv.wait_ge(A["sum"], b + 1)
                V.reciprocal(a_rsum[:, :], a_sum[:, :]).then_inc(A["rsum"], 1)

            sl = pC[:, 0:CH * (D + 1)].rearrange("p (c d) -> p c d", d=D + 1)

            def att_norms(b):
                dv.wait_ge(A["s"], b + 1)
                V.tensor_scalar(a_den[:, :], sl[:, :, D], EPS, None, ALU.add).then_inc(A["den"], 1)

            def att_token(b):
                dv.wait_ge(A["den"], b + 1)
                V.reciprocal(a_rden[:, :], a_den[:, :]).then_inc(A["rden"], 1)
                dv.wait_ge(A["rden"], b + 1)
                V.tensor_tensor(a_sn[:, :, :], sl, a_rden[:, :].unsqueeze(2).broadcast_to([P, CH, D + 1]),
                                ALU.mult).then_inc(A["sn"], 1)

            scp = pA[:, 256:256 + CH * M].rearrange("p (c m) -> p c m", m=M)

            def att_smax(b):
                dv.wait_ge(A["scp"], b + 1)
                V.tensor_reduce(a_smx[:, :], scp, AX, ALU.max).then_inc(A["smx"], 1)
                dv.wait_ge(A["smx"], b + 1)
                V.tensor_tensor(a_se[:, :, :], scp, a_smx[:, :].unsqueeze(2).broadcast_to([P, CH, M]),
                                ALU.subtract).then_inc(A["ssub"], 1)

            def att_ssum(b):
                dv.wait_ge(A["sexp"], b + 1)
                V.tensor_reduce(a_ssum[:, :], a_se[:, :, :], AX, ALU.add).then_inc(A["ssum"], 1)
                dv.wait_ge(A["ssum"], b + 1)
                V.reciprocal(a_srs[:, :], a_ssum[:, :]).then_inc(A["srs"], 1)

            def att_probs(b):
                dv.wait_ge(A["srs"], b + 1)
                V.tensor_tensor(a_at[:, :, :], a_se[:, :, :], a_srs[:, :].unsqueeze(2).broadcast_to([P, CH, M]),
                                ALU.mult).then_inc(A["at"], 1)
                dv.wait_ge(A["at"], b + 1)
                V.transpose(a_atT[:, :, :].rearrange("p c m -> p (c m)"),
                            a_at[:, :, :].rearrange("p c m -> p (c m)")).then_inc(A["atT"], 1)

            def att_residual(b):
                dv.wait_ge(A["op"], b + 1)
                hb = h_all[:, ds(b * TPB, TPB), :]
                V.tensor_tensor(hb, pB[:, 0:TPB * D].rearrange("p (t d) -> p t d", d=D), hb,
                                ALU.add).then_inc(A["h2"], 1)

            def first_eight(k, l0, l1):
                for l in range(l0, l1):
                    last = V.max(best[k][:, l, 0:8], key[:, l, :])
                return last

            def next_eight(k, l0, l1):
                for l in range(l0, l1):
                    last = V.max(best[k][:, l, 8:16], keym[:, l, :])
                return last

            def below(o, keys, eighth):
                return V.tensor_tensor(o, keys, eighth.broadcast_to(keys.shape), ALU.is_lt)

            def query_stats(b):
                dv.wait_ge(A["h2"], b + 1)
                V.memset(spare[:, 1:2], 0.0)
                for n in range(TPB):
                    last = V.bn_stats(l_st[:, n, :], h_all[:, ds(b * TPB + n, 1), :])
                last.then_inc(F["st"], 1)
                dv.wait_ge(F["st"], b + 1)
                V.memset(spare[:, 1:2], 0.0)
                for n in range(TPB):
                    last = V.bn_aggr(l_mv[:, n, :], l_st[:, n, :])
                last.then_inc(F["mv"], 1)

            def clamp_pairs(tl):
                dv.wait_ge(S["cand"], tl + 1)
                V.tensor_scalar(candc[:, :, :], cand[:, :, :].bitcast(F32), LEAST, None,
                                ALU.max).then_inc(S["clamp"], 1)

            def first_pairs(tl):
                dv.wait_ge(setup_v, 6)
                dv.wait_ge(S["clamp"], tl + 1)
                for h in range(H):
                    last = V.max(win[:, h, 0:8], candc[:, h, :])
                last.then_inc(S["wfirst"], 1)

            def mark_pairs(tl):
                dv.wait_ge(S["wfirst"], tl + 1)
                dv.wait_ge(S["wmask"], tl)
                below(candlt[:, :, :], candc[:, :, :], win[:, :, 7:8]).then_inc(S["wlt"], 1)

            def next_tokens(i, k):
                dv.wait_ge(F["rs"], i + 1 + k)
                V.tensor_scalar(x2[1 - k][:, :], h_all[:, ds(2 * i + k + 1, 1), :].squeeze(1), l_mv[:, 1 - k, 0:1],
                                l_rs[:, 1 - k:2 - k], ALU.subtract, ALU.mult).then_inc(F["x2"], 1)

            def query_squares(t0):
                dv.wait_ge(F["ssp"], t0 + 1)
                V.tensor_scalar(q_ss[:, :], pT[:, 384:384 + H], EPS, None, ALU.add).then_inc(F["ss"], 1)

            def half_squares(t0):
                dv.wait_ge(F["sq2"], t0 + 1)
                V.tensor_reduce(q_t2[:, :], q_sq2[:, :, :], AX, ALU.add).then_inc(F["t3"], 1)
                dv.wait_ge(F["t3"], t0 + 1)
                V.tensor_scalar(q_ss2[:, :], q_t2[:, :], 1e-24, None, ALU.max).then_inc(F["ss2"], 1)

            def weight_sum(kk, tp):
                dv.wait_ge(S["wexp"], tp + 1)
                V.tensor_reduce(wsum[:, :], wexp[kk][:, :, :], AX, ALU.add).then_inc(S["wsum"], 1)
                dv.wait_ge(S["wsum"], tp + 1)
                V.reciprocal(wrec[:, :], wsum[:, :]).then_inc(S["wrec"], 1)

            def result(kk, tm, before):
                dv.wait_ge(S["mix"], tm + 1)
                dv.wait_ge(stored[kk], 16 * before)
                V.tensor_tensor(res[kk][:, :], pA[:, 384:512], h_all[:, ds(tm, 1), :].squeeze(1),
                                ALU.add).then_inc(S["res"], 1)

            def slot(i, k, on):
                att, q_on, late_on, list_on, pair_on, sc_on, mix_on, next_on = on
                b, kk = i + 1, 1 - k
                lone = att and isinstance(i, int) and i < LONE
                t0, t1, tl, tp, ts, tm = (2 * i + k - n for n in range(6))
                early = pair_on and list_on and not late_on
                if lone and k == 0 and not (isinstance(b, int) and b == 0):
                    att_norm(b)
                if list_on:
                    dv.wait_ge(S["key"], tl + 1)
                    V.memset(spare[:, 0:1], 0.0)
                if list_on:
                    first_eight(k, 0, HS).then_inc(S["first"], 1)
                if att and not lone and k == 0 and not (isinstance(b, int) and b == 0):
                    att_norm(b)
                if list_on:
                    dv.wait_ge(S["first"], tl + 1)
                    dv.wait_ge(S["mask"], tl)
                    below(keylt[:, :, :], key[:, :, :], best[k][:, :, 7:8]).then_inc(S["lt"], 1)
                if lone and k == 0:
                    att_max(b)
                if q_on:
                    query_squares(t0)
                if sc_on:
                    dv.wait_ge(S["t3"], ts + 1)
                    dv.wait_ge(S["sctp"], ts)
                    dv.wait_ge(S["ohl"], ts)
                    V.tensor_tensor(ohlb[:, :, :], lo_t[:, :].unsqueeze(1).broadcast_to([P, LO, P]),
                                    lo_iota[:, :, :], ALU.is_equal).then_inc(S["ohlb"], 1)
                    for n in range(HI):
                        last = V.scalar_tensor_tensor(ohw[:, :, n, :], by_group(t3[:, 1, :]), float(n),
                                                      by_group(t3[:, 0, :]), ALU.is_equal, ALU.mult)
                    last.then_inc(S["ohw"], 1)
                if att and not lone and k == 0:
                    att_max(b)
                if held_before(i, k):
                    result(k, tm - 1, i - 3)
                if list_on:
                    dv.wait_ge(setup_v, 6)
                    dv.wait_ge(S["mask"], tl + 1)
                    next_eight(k, 0, HS // 2)
                if att and k == 0:
                    att_sub(b)
                if q_on:
                    dv.wait_ge(F["rq"], t0 + 1)
                    dv.wait_ge(F["q"], t0 + 1)
                    V.tensor_tensor(q_r[:, :, :], pS[:, 0:INNER].rearrange("p (h d) -> p h d", d=DH),
                                    q_rs[:, :].unsqueeze(2).broadcast_to([P, H, DH]), ALU.mult).then_inc(F["qr"], 1)
                if att and k == 0:
                    att_sum(b)
                    att_rsum(b)
                if list_on:
                    next_eight(k, HS // 2, HS).then_inc(S["second"], 1)
                if q_on and k == 0:
                    half_squares(t0)
                if att and k == 1:
                    att_smax(b)
                if list_on:
                    dv.wait_ge(S["second"], tl + 1)
                    V.tensor_scalar(base[k][:, :], best[k][:, :, 0].bitcast(I32), -2 ** IDX, None,
                                    ALU.bitwise_and).then_inc(S["base"], 1)
                if att and k == 1:
                    att_ssum(b)
                if pair_on:
                    dv.wait_ge(setup_v, 6)
                    dv.wait_ge(S["wmask"], tp + 1)
                    for h in range(H):
                        last = V.max(win[:, h, 8:16], candm[:, h, :])
                    last.then_inc(S["wsecond"], 1)
                if att and k == 1:
                    att_probs(b)
                if pair_on:
                    wi = win[:, :, :].bitcast(I32).rearrange("p h n -> p (h n)")
                    dv.wait_ge(S["wsecond"], tp + 1)
                    V.tensor_scalar(valb[:, :], wi, IDX, None, ALU.logical_shift_right)
                    V.tensor_scalar(hlb[:, 0, :], wi, 4, HI - 1, ALU.logical_shift_right, ALU.bitwise_and)
                    V.tensor_scalar(hlb[:, 1, :], wi, LO - 1, None, ALU.bitwise_and).then_inc(S["dec"], 1)
                if q_on and k == 1:
                    half_squares(t0)
                if early:
                    weight_sum(kk, tp)
                if list_on and k == 1:
                    clamp_pairs(tl)
                if list_on and k == 1:
                    first_pairs(tl)
                if late_on:
                    dv.wait_ge(F["y"], t1 + 1)
                    V.scalar_tensor_tensor(key[:, :, :].bitcast(I32), y[kk][:, :].rearrange("p (l e) -> p l e", e=PK),
                                           IDX, idx_iota[:, :].unsqueeze(1).broadcast_to([P, HS, PK]),
                                           ALU.logical_shift_left, ALU.bitwise_or).then_inc(S["key"], 1)
                if pair_on and not early:
                    weight_sum(kk, tp)
                if list_on and k == 1:
                    mark_pairs(tl)
                if att and k == 1:
                    att_residual(b)
                    query_stats(b)
                if att and k == 0:
                    att_norms(b)
                if mix_on and k == 0 and not held(on):
                    result(kk, tm, i - 3 + k)
                if att and k == 0:
                    att_token(b)
                if next_on and k == 0 and not (isinstance(i, int) and i <= EAGER):
                    next_tokens(i, k)
                if list_on and k == 0:
                    clamp_pairs(tl)
                if list_on and k == 0:
                    first_pairs(tl)
                    mark_pairs(tl)
                if next_on and k == 1:
                    next_tokens(i, k)
                if isinstance(i, int) and i < EAGER and k == 1:
                    next_tokens(i + 1, 0)
                if mix_on and k == 1 and not held(on):
                    result(kk, tm, i - 3 + k)

            for i in range(FIRST, LOOP0):
                for k in range(2):
                    slot(i, k, stages(i, k))
                    if i == FIRST and k == 0:
                        V.tensor_tensor(wqg[:, :, :], wqc[:, :, :], g_sb[:, :].unsqueeze(1).broadcast_to([D, H, DH]),
                                        ALU.mult)
                        V.tensor_tensor(bqg, bqc, g_sb[0:1, :].unsqueeze(1).broadcast_to([1, H, DH]),
                                        ALU.mult).then_inc(setup_t, 1)
                        split(10, 0, BLG)
                        att_stats(2, range(TPB, TILES), gathered, 16 * (TILES - TPB))
            with dv.Fori(LOOP0, LOOP1) as i:
                for k in range(2):
                    slot(i, k, stages(None, k))
            for i in range(LOOP1, LAST + 1):
                for k in range(2):
                    slot(i, k, stages(i, k))

        @block.tensor
        def _(pe):
            T = nc.tensor

            def row_bias(o, at, n):
                return T.matmul(o, pick[:, :], parts[:, at:at + n], start=False, stop=True)

            pe.wait_ge(logit_loads, 16 * len(LOGIT_LOADS))
            pe.wait_ge(pc, 2)
            for h in range(H):
                T.matmul(pA[:, h * M:(h + 1) * M], wx_sb[:, h, :], wsT_sb[:, :], start=True, stop=True)
            pe.wait_ge(setup_o, 1)
            for h in range(H):
                o = pB[0:1, h * M:(h + 1) * M]
                T.matmul(o, bxT_sb[:, h:h + 1], wsT_sb[:, :], start=True, stop=False)
                last = T.matmul(o, ones[0:1, 0:1], bsl_sb[:, :], start=False, stop=True)
            last.then_inc(setup_a, 1)
            pe.wait_ge(setup_v, 6)

            def weights():
                pe.wait_ge(query_loads, 16 * len(QUERY_LOADS))
                pe.wait_ge(other_loads, 16 * len(OTHER_LOADS))
                T.matmul(pQ[0:DH, P:P + DH], aq_sb[:, :], ak_sb[:, :], start=True, stop=True)
                T.transpose(pQ[:, 0:PK], k_unit[:, :, :, :].rearrange("p r s d -> p (r s d)"), ident[0:PK, 0:PK])
                for n in range(2):
                    T.matmul(pS[0:DH, 512 * n:512 * n + 512], av_sb[:, :], wout_sb[:, 4 * n:4 * n + 4, :],
                             start=True, stop=True)
                for c in range(4):
                    last = T.matmul(pM[:, c:c + 1], bqc_row[:, c * P:(c + 1) * P], ones[0:1, 0:1],
                                    start=True, stop=True)
                last.then_inc(setup_a, 1)

            def att_xT(b):
                pe.wait_ge(A["x"], b + 1)
                for k in range(TPB):
                    last = T.transpose(pA[:, k * P:(k + 1) * P], a_x[:, k, 0:D], ident[:, :])
                last.then_inc(A["xTp"], 1)

            def att_logits(b):
                pe.wait_ge(A["xT"], b + 1)
                for k in range(TPB):
                    o = pB[:, k * HM:(k + 1) * HM]
                    T.matmul(o, a_xT[:, k, :], lw[:, :], start=True, stop=False)
                    last = row_bias(o, BLG, HM)
                last.then_inc(A["lg"], 1)

            def att_slice(b):
                pe.wait_ge(A["sw"], b + 1)
                for c in range(CH):
                    for k in range(TPB):
                        last = T.matmul(pC[:, c * (D + 1):(c + 1) * (D + 1)], a_sw[:, k, c * P:(c + 1) * P],
                                        a_x[:, k, :], start=(k == 0), stop=(k == TPB - 1))
                last.then_inc(A["s"], 1)
                for c in range(CH):
                    for k in range(TPB):
                        last = T.transpose(pB[:, (c * TPB + k) * P:(c * TPB + k + 1) * P],
                                           a_sw[:, k, c * P:(c + 1) * P], ident[:, :])
                last.then_inc(A["swTp"], 1)

            def att_snT(b):
                pe.wait_ge(A["sn"], b + 1)
                for c in range(CH):
                    T.transpose(pA[:, c * P:(c + 1) * P], a_sn[:, c, 0:D], ident[:, :])
                    last = T.matmul(pA[0:1, 256 + c * P:256 + (c + 1) * P], a_sn[:, c, D:D + 1], ident[:, :],
                                    start=True, stop=True)
                last.then_inc(A["snTp"], 1)

            def att_st(b):
                pe.wait_ge(setup_v, 6)
                pe.wait_ge(A["snT"], b + 1)
                for h in range(H):
                    o = pC[0:DH, h * M:(h + 1) * M]
                    T.matmul(o, wfxT_sb[:, h * DH:(h + 1) * DH], a_snT[:, h * M:(h + 1) * M], start=True, stop=False)
                    last = T.matmul(o, bfx_sb[0:1, h * DH:(h + 1) * DH], a_nnT[0:1, h * M:(h + 1) * M],
                                    start=False, stop=True)
                last.then_inc(A["stp"], 1)

            def att_uv(b):
                pe.wait_ge(setup_v, 6)
                pe.wait_ge(A["stT"], b + 1)
                T.matmul(pC[0:DH, 256:512], mqk[:, :], a_stT[:, :], start=True, stop=True)
                for h in range(H):
                    c, j = divmod(h, HPC)
                    last = T.matmul(pA[32 * j:32 * j + 32, c * D:(c + 1) * D], a_stT[:, h * M:(h + 1) * M],
                                    vw[:, h, :], start=True, stop=True)
                last.then_inc(A["up"], 1)

            def att_scores(b):
                pe.wait_ge(setup_v, 6)
                pe.wait_ge(A["uT"], b + 1)
                for h in range(H):
                    c, j = divmod(h, HPC)
                    last = T.matmul(pA[32 * j:32 * j + 32, 256 + c * M:256 + (c + 1) * M],
                                    a_uT[:, h * M:(h + 1) * M], a_stT[:, h * M:(h + 1) * M], start=True, stop=True)
                last.then_inc(A["scp"], 1)

            def att_mix(b):
                pe.wait_ge(setup_v, 6)
                pe.wait_ge(A["atT"], b + 1)
                for h in range(H):
                    c, j = divmod(h, HPC)
                    last = T.matmul(pC[32 * j:32 * j + 32, c * D:(c + 1) * D], a_atT[32 * j:32 * j + 32, c, :],
                                    a_sv[32 * j:32 * j + 32, c, :], start=True, stop=True)
                last.then_inc(A["pp"], 1)

            def att_out(b):
                pe.wait_ge(A["p"], b + 1)
                for k in range(TPB):
                    o = pB[:, k * D:(k + 1) * D]
                    for c in range(CH):
                        T.matmul(o, a_swT[:, c, k * P:(k + 1) * P], a_p[:, c, :], start=(c == 0), stop=False)
                    last = row_bias(o, BOUT, D)
                last.then_inc(A["op"], 1)

            def mix_transpose(tm):
                pe.wait_ge(S["res"], tm)
                pe.wait_ge(S["act"], tm + 1)
                T.transpose(pA[:, 384:512], act[:, :], ident[:, :]).then_inc(S["actTp"], 1)

            def scatter(ts):
                pe.wait_ge(S["ohw"], ts + 1)
                pe.wait_ge(S["ohl"], ts + 1)
                for c in range(NG):
                    for j in range(4):
                        first = c * 4 + j
                        last = T.matmul(pT[32 * j:32 * j + 32, c * GRP * LO:(c + 1) * GRP * LO],
                                        ohw[:, first, :, :].rearrange("p h g -> p (h g)"),
                                        ohl[:, :, first:P:P // GRP].rearrange("p l t -> p t l"), start=True, stop=True)
                last.then_inc(S["sctp"], 1)

            def mix(tm):
                pe.wait_ge(S["actT"], tm + 1)
                T.matmul(pA[:, 384:512], actT[:, :], up_sb[:, :], start=True, stop=True).then_inc(S["mix"], 1)

            def slot(i, k, on):
                att, q_on, late_on, _, _, sc_on, mix_on, _ = on
                b = i + 1
                lone = att and isinstance(i, int) and i < LONE
                t0, t1, _, _, ts, tm = (2 * i + k - n for n in range(6))
                if q_on:
                    if k == 0:
                        pe.wait_ge(F["gate"], i)
                    pe.wait_ge(F["x2"], t0 + 1)
                    T.transpose(pM[:, 0:P], x2[k][:, :], ident[:, :]).then_inc(F["x2Tp"], 1)
                if sc_on:
                    pe.wait_ge(S["wn"], ts + 1)
                    pe.wait_ge(S["hl"], ts + 1)
                    if late_on:
                        pe.wait_ge(S["sct"], ts)
                    else:
                        pe.wait_ge(S["t3"], ts)
                    bank = triples(on)
                    T.transpose(bank[:, 0:P], wn[:, :, :].rearrange("p h n -> p (h n)"), ident[:, :])
                    for n in range(2):
                        last = T.transpose(bank[:, (n + 1) * P:(n + 2) * P], hl[k][:, n, :], ident[:, :])
                    last.then_inc(S["t3p"], 1)
                if held_before(i, k):
                    mix_transpose(tm - 1)
                    mix(tm - 1)
                if lone and k == 0:
                    if mix_on:
                        pe.wait_ge(S["res"], tm)
                    att_xT(b)
                if att and k == 1 and mix_on:
                    pe.wait_ge(S["res"], tm)
                if lone and k == 0:
                    att_logits(b)
                if q_on:
                    pe.wait_ge(F["x2T"], t0 + 1)
                    for c in range(4):
                        last = T.matmul(pQ[:, c * P:(c + 1) * P], wqc[:, 2 * c:2 * c + 2, :].rearrange("p h d -> p (h d)"),
                                        x2T[k][:, :], start=True, stop=True)
                    last.then_inc(F["qc"], 1)
                if q_on:
                    if late_on:
                        pe.wait_ge(F["y"], t1)
                    T.matmul(pS[:, 0:INNER], x2T[k][:, :], wqg[:, :, :], start=True, stop=False)
                    row_bias(pS[:, 0:INNER], BQG, INNER).then_inc(F["q"], 1)
                    T.matmul(pM[:, P + k * P:2 * P + k * P], x2T[k][:, :], downT_sb[:, :],
                             start=True, stop=True).then_inc(F["inner"], 1)
                    pe.wait_ge(F["sq"], t0 + 1)
                    pe.wait_ge(F["ss"], t0)
                    if sc_on:
                        pe.wait_ge(S["t3"], ts + 1)
                    for c in range(4):
                        last = T.matmul(pT[:, 384 + 2 * c:386 + 2 * c], q_sq[:, c, :], half_c[:, :], start=True, stop=True)
                    last.then_inc(F["ssp"], 1)
                if att and not lone and k == 0:
                    if mix_on:
                        pe.wait_ge(S["res"], tm)
                    att_xT(b)
                if att and k == 1:
                    att_st(b)
                if att and k == 1:
                    att_uv(b)
                if late_on:
                    pe.wait_ge(F["qn"], t1 + 1)
                    if q_on:
                        pe.wait_ge(F["sq"], t0 + 1)
                    for c in range(4):
                        last = T.transpose(pQ[:, c * P:(c + 1) * P],
                                           q_n[:, 4 * c:4 * c + 4, :].rearrange("p l d -> p (l d)"), ident[:, :])
                    last.then_inc(F["qnTp"], 1)
                if att and k == 1:
                    att_scores(b)
                if att and not lone and k == 0:
                    att_logits(b)
                if sc_on and q_on and k == 0:
                    scatter(ts)
                if late_on:
                    pe.wait_ge(F["qnT"], t1 + 1)
                    if q_on:
                        pe.wait_ge(F["qr"], t0 + 1)
                    for c in range(4):
                        for n in range(2):
                            at = (n * 4 + c) * 2 * PK
                            last = T.matmul(pS[:, at:at + 2 * PK], q_nT[64 * n:64 * n + 64, c, :],
                                            kb[64 * n:64 * n + 64, :, :], start=True, stop=True)
                    last.then_inc(F["sc"], 1)
                if att and k == 1:
                    att_mix(b)
                if sc_on and not q_on:
                    scatter(ts)
                if mix_on and not held(on):
                    mix_transpose(tm)
                if att and k == 1:
                    att_out(b)
                if sc_on and q_on and k == 1:
                    scatter(ts)
                if mix_on and not held(on):
                    mix(tm)
                if isinstance(i, int) and i == FIRST and k == 0:
                    weights()
                if att and k == 0:
                    att_slice(b)
                if att and k == 0:
                    if mix_on:
                        pe.wait_ge(S["res"], tm + 1)
                    att_snT(b)

            for i in range(FIRST, LOOP0):
                for k in range(2):
                    if i == FIRST and k == 1:
                        pe.wait_ge(setup_b, 1)
                    if i == 0 and k == 0:
                        pe.wait_ge(setup_v, 7)
                    slot(i, k, stages(i, k))
            with pe.Fori(LOOP0, LOOP1) as i:
                for k in range(2):
                    slot(i, k, stages(None, k))
            for i in range(LOOP1, LAST + 1):
                for k in range(2):
                    slot(i, k, stages(i, k))

        @block.scalar
        def _(ac):
            C = nc.scalar

            def copy(o, i_):
                return C.activation(o, i_, ACT.Copy)

            for dst, src in QUERY_LOADS:
                ac.dma_start(dst, src).then_inc(query_loads, 16)

            def weights():
                ac.wait_ge(setup_a, 2)
                copy(mqk[:, :], pQ[0:DH, P:P + DH])
                for n in range(4):
                    copy(kb[32 * n:32 * n + 32, n % 2, :], pQ[32 * n:32 * n + 32, 0:PK])
                for n in range(2):
                    copy(vw[:, 4 * n:4 * n + 4, :].rearrange("p h o -> p (h o)"), pS[0:DH, 512 * n:512 * n + 512])
                copy(bqcT[:, :], pM[:, 0:4]).then_inc(setup_b, 1)

            def att_xT(b):
                ac.wait_ge(A["xTp"], b + 1)
                copy(a_xT[:, :, :].rearrange("p t n -> p (t n)"), pA[:, 0:TPB * P]).then_inc(A["xT"], 1)

            def att_exp(b):
                ac.wait_ge(A["sub"], b + 1)
                C.activation(a_e[:, :, :], a_e[:, :, :], ACT.Exp).then_inc(A["exp"], 1)

            def att_swT(b):
                ac.wait_ge(A["swTp"], b + 1)
                copy(a_swT[:, :, :].rearrange("p c n -> p (c n)"), pB[:, :]).then_inc(A["swT"], 1)

            def att_snT(b):
                ac.wait_ge(A["snTp"], b + 1)
                copy(a_snT[:, :], pA[:, 0:HM])
                copy(a_nnT[:, :], pA[0:1, 256:256 + HM]).then_inc(A["snT"], 1)

            def att_stT(b):
                ac.wait_ge(A["stp"], b + 1)
                copy(a_stT[:, :], pC[0:DH, 0:HM]).then_inc(A["stT"], 1)

            def att_uT(b):
                ac.wait_ge(A["up"], b + 1)
                copy(a_uT[:, :], pC[0:DH, 256:512])
                copy(a_sv[:, :, :].rearrange("p c d -> p (c d)"), pA[:, 0:CH * D]).then_inc(A["uT"], 1)

            def att_sexp(b):
                ac.wait_ge(A["ssub"], b + 1)
                C.activation(a_se[:, :, :], a_se[:, :, :], ACT.Exp, scale=DH ** -0.5).then_inc(A["sexp"], 1)

            def att_p(b):
                ac.wait_ge(A["pp"], b + 1)
                copy(a_p[:, :, :].rearrange("p c d -> p (c d)"), pC[:, 0:CH * D]).then_inc(A["p"], 1)

            def scattered(ts):
                ac.wait_ge(S["sctp"], ts + 1)
                ac.wait_ge(spilled, 16 * GRP * ts)
                copy(sct[:, :, :].rearrange("p c n -> p (c n)"), pT[:, :]).then_inc(S["sct"], 1)

            def low_rows(ts):
                ac.wait_ge(S["ohlb"], ts + 1)
                ac.wait_ge(S["sctp"], ts)
                copy(ohl[:, :, :].rearrange("p l t -> p (l t)"),
                     ohlb[:, :, :].rearrange("p l t -> p (l t)")).then_inc(S["ohl"], 1)

            def winners(kk, tp):
                ac.wait_ge(S["dec"], tp + 1)
                C.activation(wexp[kk][:, :, :].rearrange("p h n -> p (h n)"), valb[:, :], ACT.Exp,
                             bias=exp_bias[:, :], scale=1.0 / UNIT).then_inc(S["wexp"], 1)
                copy(hl[kk][:, :, :].rearrange("p n j -> p (n j)"),
                     hlb[:, :, :].rearrange("p n j -> p (n j)")).then_inc(S["hl"], 1)

            def mixed(tm):
                ac.wait_ge(S["actTp"], tm + 1)
                copy(actT[:, :], pA[:, 384:512]).then_inc(S["actT"], 1)

            def slot(i, k, on):
                att, q_on, late_on, list_on, pair_on, sc_on, mix_on, _ = on
                b, kk = i + 1, 1 - k
                lone = att and isinstance(i, int) and i < LONE
                t0, t1, _, tp, ts, tm = (2 * i + k - n for n in range(6))
                if q_on:
                    ac.wait_ge(F["x2Tp"], t0 + 1)
                    copy(x2T[k][:, :], pM[:, 0:P]).then_inc(F["x2T"], 1)
                if sc_on:
                    ac.wait_ge(S["t3p"], ts + 1)
                    ac.wait_ge(S["ohlb"], ts)
                    copy(t3[:, :, :].rearrange("p n t -> p (n t)"), triples(on)[:, 0:2 * P])
                    copy(lo_t[:, :], triples(on)[:, 2 * P:3 * P]).then_inc(S["t3"], 1)
                if held_before(i, k):
                    mixed(tm - 1)
                if lone and k == 0:
                    att_xT(b)
                if q_on:
                    ac.wait_ge(F["qc"], t0 + 1)
                    for c in range(4):
                        last = C.activation(q_sq[:, c, :], pQ[:, c * P:(c + 1) * P], ACT.Square, bias=bqcT[:, c:c + 1])
                    last.then_inc(F["sq"], 1)
                if q_on and k == 1:
                    ac.wait_ge(F["inner"], t0 + 1)
                    C.activation(gate[:, ds(t0 - 1, 2), :].rearrange("p t e -> p (t e)"), pM[:, P:3 * P],
                                 ACT.Gelu).then_inc(F["gate"], 1)
                    C.activation(warm[:, :], exp_bias[:, :], ACT.Exp)
                if att and k == 1:
                    att_stT(b)
                if att and not lone and k == 0:
                    att_xT(b)
                if att and k == 1:
                    att_uT(b)
                if late_on:
                    ac.wait_ge(F["qnTp"], t1 + 1)
                    copy(q_nT[:, :, :].rearrange("p c t -> p (c t)"), pQ[:, :]).then_inc(F["qnT"], 1)
                if att and k == 1:
                    att_sexp(b)
                if sc_on and (k == 0 or not q_on):
                    low_rows(ts)
                if att and k == 0:
                    att_exp(b)
                if q_on:
                    ac.wait_ge(F["q1"], t0 + 1)
                    C.activation(q_sq2[:, :, :].rearrange("p l d -> p (l d)"),
                                 q_1[:, :, :].rearrange("p h d -> p (h d)"), ACT.Square).then_inc(F["sq2"], 1)
                if sc_on and q_on and k == 0:
                    scattered(ts)
                if sc_on and q_on and k == 1:
                    low_rows(ts)
                if pair_on and not list_on:
                    winners(kk, tp)
                if pair_on and list_on and not q_on and not late_on:
                    winners(kk, tp)
                if late_on:
                    ac.wait_ge(F["sc"], t1 + 1)
                    for n in range(2):
                        last = C.activation(y[kk][:, n * 512:(n + 1) * 512], pS[:, n * 512:(n + 1) * 512],
                                            ACT.Identity, bias=one_bias[:, :], scale=UNIT)
                    last.then_inc(F["y"], 1)
                if sc_on and not q_on:
                    scattered(ts)
                if pair_on and late_on and not q_on:
                    winners(kk, tp)
                if att and k == 1:
                    att_p(b)
                if mix_on and not held(on):
                    mixed(tm)
                if pair_on and q_on:
                    winners(kk, tp)
                if sc_on and q_on and k == 1:
                    scattered(ts)
                if isinstance(i, int) and i == FIRST and k == 0:
                    weights()
                if att and k == 0:
                    att_swT(b)
                if att and k == 0:
                    att_snT(b)

            for i in range(FIRST, LOOP0):
                for k in range(2):
                    slot(i, k, stages(i, k))
            with ac.Fori(LOOP0, LOOP1) as i:
                for k in range(2):
                    slot(i, k, stages(None, k))
            for i in range(LOOP1, LAST + 1):
                for k in range(2):
                    slot(i, k, stages(i, k))


def kernel(**inputs):
    import numpy as np
    import concourse.bacc as bacc
    from concourse import mybir as mb
    from concourse.bass_utils import run_bass_kernel_spmd

    a = {n: np.asarray(v) for n, v in inputs.items()}
    x = a["x"].astype(np.int32)
    B, N = x.shape
    D = a["L0_tok_weight"].shape[1]
    P, DH, PK = 128, a["L0_attn_Wslice"].shape[1], a["L0_ffn_keys0"].shape[0]
    arrays = [
        ("ids", x.reshape(-1, P).T), ("tok", a["L0_tok_weight"]), ("wx", a["L0_attn_Wx"]), ("wfxT", a["L0_attn_Wfx"].T),
        ("wsT", a["L0_attn_Wslice"].T), ("bxT", a["L0_attn_bx"].reshape(-1, DH).T), ("bfx", a["L0_attn_bfx"][None]),
        ("bslice", a["L0_attn_bslice"][None]), ("attn_wq", a["L0_attn_Wq"]), ("attn_wk", a["L0_attn_Wk"]),
        ("attn_wv", a["L0_attn_Wv"]), ("woutT", a["L0_attn_Wout"].T), ("bout", a["L0_attn_bout"][None]),
        ("temperature", a["L0_attn_temperature"].reshape(1, -1)), ("ffn_wqT", a["L0_ffn_Wq"].T),
        ("bq", a["L0_ffn_bq"][None]), ("ln_g", a["L0_ffn_ln_g"][None]), ("ln_b", a["L0_ffn_ln_b"][None]),
        ("keys0", a["L0_ffn_keys0"]), ("keys1", a["L0_ffn_keys1"]), ("downT", a["L0_ffn_expert_down"][:2 * PK].T),
        ("up", a["L0_ffn_expert_up"]),
    ]
    nc = bacc.Bacc("TRN2", target_bir_lowering=False, num_devices=1)
    feed, args = {}, []
    for name, v in arrays:
        v = np.ascontiguousarray(v)
        feed[name + "_dram"] = v
        args.append(nc.dram_tensor(name + "_dram", v.shape, mb.dt.from_np(v.dtype), kind="ExternalInput").ap())
    args.append(nc.dram_tensor("out_dram", (B * N, D), mb.dt.float32, kind="ExternalOutput").ap())
    tower_program(nc, *args)
    r = run_bass_kernel_spmd(nc, [feed], core_ids=[0])
    return r.results[0]["out_dram"].reshape(B, N, D)
```
